# Optimizing a Trainium2 kernel written in Bass

```python
import numpy as np
import jax
import jax.numpy as jnp

def _softmax(x, axis=-1):
    return jax.nn.softmax(x, axis=axis)

def _gelu(x):
    return jax.nn.gelu(x, approximate=True)

def _silu(x):
    return jax.nn.silu(x)

def _sigmoid(x):
    return jax.nn.sigmoid(x)

def _layernorm(x, axis=-1, eps=1e-05):
    m = jnp.mean(x, axis=axis, keepdims=True)
    v = jnp.var(x, axis=axis, keepdims=True)
    return (x - m) / jnp.sqrt(v + eps)

def _scatter_add(tgt, idx, src, axis=0):
    return tgt.at[idx].add(src)

def _segment_sum(src, seg, n):
    return jax.ops.segment_sum(src, seg, n)
kernel_name = 'mk_xattn_seq_d2_seqx_r4_084585'

def setup_inputs(seed: int=0):
    np.random.seed(seed)
    _w = jnp.asarray

    def _rec_inputs():
        import jax
        import jax.numpy as jnp
        _rk = jax.random.key(seed)
        x = 7.22e-05 + 1 * jax.random.normal(jax.random.fold_in(_rk, 1), (8, 112, 512), jnp.float32)
        _lenS = 112 - jax.random.randint(jax.random.fold_in(_rk, 7), (8,), 0, max(1, 112 // 4) + 1, jnp.int32)
        _lenS2 = 375 - jax.random.randint(jax.random.fold_in(_rk, 8), (8,), 0, max(1, 375 // 4) + 1, jnp.int32)
        _ctx_2048P = jax.random.normal(jax.random.fold_in(_rk, 11), (8, 16, 512), jnp.float32)
        _ctx_2048c = jax.random.dirichlet(jax.random.fold_in(_rk, 511), 0.3 * jnp.ones((16,), jnp.float32), (8, 375))
        _ctx_2048t = jnp.einsum('bsk,bkd->bsd', _ctx_2048c, _ctx_2048P)
        _ctx_2048t = _ctx_2048t * jax.lax.rsqrt(jnp.mean(jnp.square(_ctx_2048t)) + 1e-12) * 0.953939
        ctx_2048 = 3.03215e-05 + 0.0999827 * (_ctx_2048t + 0.3 * jax.random.normal(jax.random.fold_in(_rk, 611), (8, 375, 512), jnp.float32))
        _validS = jnp.arange(112)[None, :] < _lenS[:, None]
        _validS2 = jnp.arange(375)[None, :] < _lenS2[:, None]
        _causal = jnp.tril(jnp.ones((112, 112), dtype=bool))
        mask_BxS2_ik0 = jnp.where(jnp.broadcast_to(_validS2[:, :], (8, 375)), 0, 1).astype(jnp.int32)
        return (x, ctx_2048, mask_BxS2_ik0)
    x, ctx_2048, mask_BxS2_ik0 = _rec_inputs()

    def _L0_xattn_setup():
        import jax, jax.numpy as jnp
        import numpy as np
        N_HEAD = 32
        EPS = 1e-05

        def _ln(x, w, b):
            m = jnp.mean(x, axis=-1, keepdims=True)
            v = jnp.mean((x - m) ** 2, axis=-1, keepdims=True)
            return (x - m) * jax.lax.rsqrt(v + EPS) * w + b

        def _forward(x, state, i, ln1_w, ln1_b, ln2_w, ln2_b, maa_x, maa_w, maa_k, maa_v, maa_r, maa_g, maa_w1, maa_w2, time_decay, decay_w1, decay_w2, faaaa, Wr, Wk, Wv, Wg, Wo, gn_w, gn_b, fmaa_k, fmaa_r, fWk, fWr, fWv):
            B, L, C = x.shape
            H = N_HEAD
            S = C // H
            i0 = (2 + S) * i
            xa = _ln(x, ln1_w, ln1_b)
            sx = jnp.concatenate([state[:, i0 + 1][:, None], xa[:, :-1]], axis=1) - xa
            xxx = xa + sx * maa_x
            t = jnp.tanh(xxx @ maa_w1).reshape(B, L, 5, -1)
            m = jnp.einsum('blfd,fdc->blfc', t, maa_w2)
            mw, mk, mv, mr, mg = (m[:, :, j] for j in range(5))
            xw = xa + sx * (maa_w + mw)
            xk = xa + sx * (maa_k + mk)
            xv = xa + sx * (maa_v + mv)
            xr = xa + sx * (maa_r + mr)
            xg = xa + sx * (maa_g + mg)
            w = time_decay + jnp.tanh(xw @ decay_w1) @ decay_w2
            w = jnp.exp(-jnp.exp(w)).reshape(B, L, H, S)
            r = (xr @ Wr.T).reshape(B, L, H, S)
            k = (xk @ Wk.T).reshape(B, L, H, S)
            v = (xv @ Wv.T).reshape(B, L, H, S)
            g = jax.nn.silu(xg @ Wg.T)
            s0 = state[:, i0 + 2:i0 + 2 + S].reshape(B, H, S, S)

            def step(s, inp):
                k_l, v_l, w_l, r_l = inp
                a = k_l[..., :, None] * v_l[..., None, :]
                out = jnp.einsum('bhs,bhst->bht', r_l, faaaa * a + s)
                s_new = a + w_l[..., None] * s
                return (s_new, out)
            seq = tuple((z.transpose(1, 0, 2, 3) for z in (k, v, w, r)))
            _, outs = jax.lax.scan(step, s0, seq)
            y = outs.transpose(1, 0, 2, 3)
            gm = jnp.mean(y, axis=-1, keepdims=True)
            gv = jnp.mean((y - gm) ** 2, axis=-1, keepdims=True)
            y = ((y - gm) * jax.lax.rsqrt(gv + EPS)).reshape(B, L, C) * gn_w + gn_b
            x = x + y * g @ Wo.T
            xc = _ln(x, ln2_w, ln2_b)
            sxc = jnp.concatenate([state[:, i0][:, None], xc[:, :-1]], axis=1) - xc
            xk2 = xc + sxc * fmaa_k
            xr2 = xc + sxc * fmaa_r
            rr = jax.nn.sigmoid(xr2 @ fWr.T)
            kk = jnp.square(jax.nn.relu(xk2 @ fWk.T))
            x = x + rr * (kk @ fWv.T)
            return x
        key = jax.random.key(seed)
        B, L, C, H = (8, 128, 512, N_HEAD)
        S = C // H
        DM, DD = (32, 64)
        ks = jax.random.split(key, 32)
        n = lambda k, shp, s=1.0: jax.random.normal(k, shp, dtype=jnp.float32) * s
        u = lambda k, shp: jax.random.uniform(k, shp, dtype=jnp.float32)
        inp = {'x': n(ks[0], (B, L, C)), 'state': n(ks[1], (B, 2 + S, C), 0.1), 'i': 0, 'ln1_w': jnp.ones((C,), jnp.float32), 'ln1_b': jnp.zeros((C,), jnp.float32), 'ln2_w': jnp.ones((C,), jnp.float32), 'ln2_b': jnp.zeros((C,), jnp.float32), 'maa_x': u(ks[2], (C,)), 'maa_w': u(ks[3], (C,)), 'maa_k': u(ks[4], (C,)), 'maa_v': u(ks[5], (C,)), 'maa_r': u(ks[6], (C,)), 'maa_g': u(ks[7], (C,)), 'maa_w1': n(ks[8], (C, 5 * DM), 0.02), 'maa_w2': n(ks[9], (5, DM, C), 0.02), 'time_decay': n(ks[10], (C,), 0.5), 'decay_w1': n(ks[11], (C, DD), 0.02), 'decay_w2': n(ks[12], (DD, C), 0.02), 'faaaa': n(ks[13], (H, S, 1), 0.1), 'Wr': n(ks[14], (C, C), 0.02), 'Wk': n(ks[15], (C, C), 0.02), 'Wv': n(ks[16], (C, C), 0.02), 'Wg': n(ks[17], (C, C), 0.02), 'Wo': n(ks[18], (C, C), 0.02), 'gn_w': jnp.ones((C,), jnp.float32), 'gn_b': jnp.zeros((C,), jnp.float32), 'fmaa_k': u(ks[19], (C,)), 'fmaa_r': u(ks[20], (C,)), 'fWk': n(ks[21], (C, C), 0.02), 'fWr': n(ks[22], (C, C), 0.02), 'fWv': n(ks[23], (C, C), 0.02)}
        return inp
    _L0_xattn_all = _L0_xattn_setup()
    _L0_xattn_in = {k: v for k, v in _L0_xattn_all.items() if k in ('ln1_w', 'ln1_b', 'ln2_w', 'ln2_b', 'maa_x', 'maa_w', 'maa_k', 'maa_v', 'maa_r', 'maa_g', 'maa_w1', 'maa_w2', 'time_decay', 'decay_w1', 'decay_w2', 'faaaa', 'Wr', 'Wk', 'Wv', 'Wg', 'Wo', 'gn_w', 'gn_b', 'fmaa_k', 'fmaa_r', 'fWk', 'fWr', 'fWv')}
    del _L0_xattn_all

    def _L1_xattn_setup():
        import jax, jax.numpy as jnp
        import numpy as np
        B, P, K, H, NH = (4, 512, 64, 512, 16)
        DH = H // NH
        EPS = 1e-06

        def rmsnorm(x, w):
            var = jnp.mean(jnp.square(x), axis=-1, keepdims=True)
            return x * jax.lax.rsqrt(var + EPS) * w
        key = jax.random.key(seed)
        ks = jax.random.split(key, 12)
        s = 0.02
        return {'x': jax.random.normal(ks[0], (B, P, H), jnp.float32), 'latents': jax.random.normal(ks[1], (B, K, H), jnp.float32), 'attention_mask': jax.random.randint(ks[2], (B, P), 0, 2, jnp.int32), 'q_w': s * jax.random.normal(ks[3], (H, H), jnp.float32), 'q_b': jnp.zeros((H,), jnp.float32), 'kv_w': s * jax.random.normal(ks[4], (H, 2 * H), jnp.float32), 'kv_b': jnp.zeros((2 * H,), jnp.float32), 'out_w': s * jax.random.normal(ks[5], (H, H), jnp.float32), 'out_b': jnp.zeros((H,), jnp.float32), 'postnorm_w': jnp.ones((H,), jnp.float32), 'mlp_w1': s * jax.random.normal(ks[6], (H, 4 * H), jnp.float32), 'mlp_b1': jnp.zeros((4 * H,), jnp.float32), 'mlp_w2': s * jax.random.normal(ks[7], (4 * H, H), jnp.float32), 'mlp_b2': jnp.zeros((H,), jnp.float32)}
    _L1_xattn_all = _L1_xattn_setup()
    _L1_xattn_in = {k: v for k, v in _L1_xattn_all.items() if k in ('q_w', 'q_b', 'kv_w', 'kv_b', 'out_w', 'out_b', 'postnorm_w', 'mlp_w1', 'mlp_b1', 'mlp_w2', 'mlp_b2')}
    del _L1_xattn_all
    return {'x': x, 'ctx_2048': ctx_2048, 'mask_BxS2_ik0': mask_BxS2_ik0, 'L0_xattn_ln1_w': _L0_xattn_in['ln1_w'], 'L0_xattn_ln1_b': _L0_xattn_in['ln1_b'], 'L0_xattn_ln2_w': _L0_xattn_in['ln2_w'], 'L0_xattn_ln2_b': _L0_xattn_in['ln2_b'], 'L0_xattn_maa_x': _L0_xattn_in['maa_x'], 'L0_xattn_maa_w': _L0_xattn_in['maa_w'], 'L0_xattn_maa_k': _L0_xattn_in['maa_k'], 'L0_xattn_maa_v': _L0_xattn_in['maa_v'], 'L0_xattn_maa_r': _L0_xattn_in['maa_r'], 'L0_xattn_maa_g': _L0_xattn_in['maa_g'], 'L0_xattn_maa_w1': _L0_xattn_in['maa_w1'], 'L0_xattn_maa_w2': _L0_xattn_in['maa_w2'], 'L0_xattn_time_decay': _L0_xattn_in['time_decay'], 'L0_xattn_decay_w1': _L0_xattn_in['decay_w1'], 'L0_xattn_decay_w2': _L0_xattn_in['decay_w2'], 'L0_xattn_faaaa': _L0_xattn_in['faaaa'], 'L0_xattn_Wr': _L0_xattn_in['Wr'], 'L0_xattn_Wk': _L0_xattn_in['Wk'], 'L0_xattn_Wv': _L0_xattn_in['Wv'], 'L0_xattn_Wg': _L0_xattn_in['Wg'], 'L0_xattn_Wo': _L0_xattn_in['Wo'], 'L0_xattn_gn_w': _L0_xattn_in['gn_w'], 'L0_xattn_gn_b': _L0_xattn_in['gn_b'], 'L0_xattn_fmaa_k': _L0_xattn_in['fmaa_k'], 'L0_xattn_fmaa_r': _L0_xattn_in['fmaa_r'], 'L0_xattn_fWk': _L0_xattn_in['fWk'], 'L0_xattn_fWr': _L0_xattn_in['fWr'], 'L0_xattn_fWv': _L0_xattn_in['fWv'], 'L1_xattn_q_w': _L1_xattn_in['q_w'], 'L1_xattn_q_b': _L1_xattn_in['q_b'], 'L1_xattn_kv_w': _L1_xattn_in['kv_w'], 'L1_xattn_kv_b': _L1_xattn_in['kv_b'], 'L1_xattn_out_w': _L1_xattn_in['out_w'], 'L1_xattn_out_b': _L1_xattn_in['out_b'], 'L1_xattn_postnorm_w': _L1_xattn_in['postnorm_w'], 'L1_xattn_mlp_w1': _L1_xattn_in['mlp_w1'], 'L1_xattn_mlp_b1': _L1_xattn_in['mlp_b1'], 'L1_xattn_mlp_w2': _L1_xattn_in['mlp_w2'], 'L1_xattn_mlp_b2': _L1_xattn_in['mlp_b2']}

def reference(x, ctx_2048, mask_BxS2_ik0, L0_xattn_ln1_w, L0_xattn_ln1_b, L0_xattn_ln2_w, L0_xattn_ln2_b, L0_xattn_maa_x, L0_xattn_maa_w, L0_xattn_maa_k, L0_xattn_maa_v, L0_xattn_maa_r, L0_xattn_maa_g, L0_xattn_maa_w1, L0_xattn_maa_w2, L0_xattn_time_decay, L0_xattn_decay_w1, L0_xattn_decay_w2, L0_xattn_faaaa, L0_xattn_Wr, L0_xattn_Wk, L0_xattn_Wv, L0_xattn_Wg, L0_xattn_Wo, L0_xattn_gn_w, L0_xattn_gn_b, L0_xattn_fmaa_k, L0_xattn_fmaa_r, L0_xattn_fWk, L0_xattn_fWr, L0_xattn_fWv, L1_xattn_q_w, L1_xattn_q_b, L1_xattn_kv_w, L1_xattn_kv_b, L1_xattn_out_w, L1_xattn_out_b, L1_xattn_postnorm_w, L1_xattn_mlp_w1, L1_xattn_mlp_b1, L1_xattn_mlp_w2, L1_xattn_mlp_b2):
    import jax
    import jax.numpy as jnp

    def _L0_xattn_ref(x, state, i, ln1_w, ln1_b, ln2_w, ln2_b, maa_x, maa_w, maa_k, maa_v, maa_r, maa_g, maa_w1, maa_w2, time_decay, decay_w1, decay_w2, faaaa, Wr, Wk, Wv, Wg, Wo, gn_w, gn_b, fmaa_k, fmaa_r, fWk, fWr, fWv):
        import jax, jax.numpy as jnp
        import numpy as np
        N_HEAD = 32
        EPS = 1e-05

        def _ln(x, w, b):
            m = jnp.mean(x, axis=-1, keepdims=True)
            v = jnp.mean((x - m) ** 2, axis=-1, keepdims=True)
            return (x - m) * jax.lax.rsqrt(v + EPS) * w + b

        def _forward(x, state, i, ln1_w, ln1_b, ln2_w, ln2_b, maa_x, maa_w, maa_k, maa_v, maa_r, maa_g, maa_w1, maa_w2, time_decay, decay_w1, decay_w2, faaaa, Wr, Wk, Wv, Wg, Wo, gn_w, gn_b, fmaa_k, fmaa_r, fWk, fWr, fWv):
            B, L, C = x.shape
            H = N_HEAD
            S = C // H
            i0 = (2 + S) * i
            xa = _ln(x, ln1_w, ln1_b)
            sx = jnp.concatenate([state[:, i0 + 1][:, None], xa[:, :-1]], axis=1) - xa
            xxx = xa + sx * maa_x
            t = jnp.tanh(xxx @ maa_w1).reshape(B, L, 5, -1)
            m = jnp.einsum('blfd,fdc->blfc', t, maa_w2)
            mw, mk, mv, mr, mg = (m[:, :, j] for j in range(5))
            xw = xa + sx * (maa_w + mw)
            xk = xa + sx * (maa_k + mk)
            xv = xa + sx * (maa_v + mv)
            xr = xa + sx * (maa_r + mr)
            xg = xa + sx * (maa_g + mg)
            w = time_decay + jnp.tanh(xw @ decay_w1) @ decay_w2
            w = jnp.exp(-jnp.exp(w)).reshape(B, L, H, S)
            r = (xr @ Wr.T).reshape(B, L, H, S)
            k = (xk @ Wk.T).reshape(B, L, H, S)
            v = (xv @ Wv.T).reshape(B, L, H, S)
            g = jax.nn.silu(xg @ Wg.T)
            s0 = state[:, i0 + 2:i0 + 2 + S].reshape(B, H, S, S)

            def step(s, inp):
                k_l, v_l, w_l, r_l = inp
                a = k_l[..., :, None] * v_l[..., None, :]
                out = jnp.einsum('bhs,bhst->bht', r_l, faaaa * a + s)
                s_new = a + w_l[..., None] * s
                return (s_new, out)
            seq = tuple((z.transpose(1, 0, 2, 3) for z in (k, v, w, r)))
            _, outs = jax.lax.scan(step, s0, seq)
            y = outs.transpose(1, 0, 2, 3)
            gm = jnp.mean(y, axis=-1, keepdims=True)
            gv = jnp.mean((y - gm) ** 2, axis=-1, keepdims=True)
            y = ((y - gm) * jax.lax.rsqrt(gv + EPS)).reshape(B, L, C) * gn_w + gn_b
            x = x + y * g @ Wo.T
            xc = _ln(x, ln2_w, ln2_b)
            sxc = jnp.concatenate([state[:, i0][:, None], xc[:, :-1]], axis=1) - xc
            xk2 = xc + sxc * fmaa_k
            xr2 = xc + sxc * fmaa_r
            rr = jax.nn.sigmoid(xr2 @ fWr.T)
            kk = jnp.square(jax.nn.relu(xk2 @ fWk.T))
            x = x + rr * (kk @ fWv.T)
            return x
        return _forward(x, state, i, ln1_w, ln1_b, ln2_w, ln2_b, maa_x, maa_w, maa_k, maa_v, maa_r, maa_g, maa_w1, maa_w2, time_decay, decay_w1, decay_w2, faaaa, Wr, Wk, Wv, Wg, Wo, gn_w, gn_b, fmaa_k, fmaa_r, fWk, fWr, fWv)

    def _L1_xattn_ref(x, latents, attention_mask, q_w, q_b, kv_w, kv_b, out_w, out_b, postnorm_w, mlp_w1, mlp_b1, mlp_w2, mlp_b2):
        import jax, jax.numpy as jnp
        import numpy as np
        B, P, K, H, NH = (4, 512, 64, 512, 16)
        DH = H // NH
        EPS = 1e-06

        def rmsnorm(x, w):
            var = jnp.mean(jnp.square(x), axis=-1, keepdims=True)
            return x * jax.lax.rsqrt(var + EPS) * w
        b, p, _ = x.shape
        k_len = latents.shape[1]
        residual = latents
        h = jnp.concatenate([x, latents], axis=1)
        q = (latents @ q_w + q_b).reshape(b, k_len, NH, DH)
        kv = (h @ kv_w + kv_b).reshape(b, p + k_len, NH, DH, 2)
        kmat, v = (kv[..., 0], kv[..., 1])
        attn = jnp.einsum('bkhd,bnhd->bhkn', q, kmat) / DH
        full_mask = jnp.concatenate([attention_mask.astype(bool), jnp.ones((b, k_len), bool)], axis=-1)
        attn = jnp.where(full_mask[:, None, None, :], attn, -jnp.inf)
        attn = jax.nn.softmax(attn.astype(jnp.float32), axis=-1).astype(q.dtype)
        attn_out = jnp.einsum('bhkn,bnhd->bkhd', attn, v).reshape(b, k_len, H)
        attn_out = attn_out @ out_w + out_b + residual
        out = rmsnorm(attn_out, postnorm_w)
        out = jax.nn.gelu(out @ mlp_w1 + mlp_b1) @ mlp_w2 + mlp_b2
        return out + residual
    x = _L0_xattn_ref(x, ctx_2048, 0, L0_xattn_ln1_w, L0_xattn_ln1_b, L0_xattn_ln2_w, L0_xattn_ln2_b, L0_xattn_maa_x, L0_xattn_maa_w, L0_xattn_maa_k, L0_xattn_maa_v, L0_xattn_maa_r, L0_xattn_maa_g, L0_xattn_maa_w1, L0_xattn_maa_w2, L0_xattn_time_decay, L0_xattn_decay_w1, L0_xattn_decay_w2, L0_xattn_faaaa, L0_xattn_Wr, L0_xattn_Wk, L0_xattn_Wv, L0_xattn_Wg, L0_xattn_Wo, L0_xattn_gn_w, L0_xattn_gn_b, L0_xattn_fmaa_k, L0_xattn_fmaa_r, L0_xattn_fWk, L0_xattn_fWr, L0_xattn_fWv)
    x = _L1_xattn_ref(ctx_2048, x, mask_BxS2_ik0, L1_xattn_q_w, L1_xattn_q_b, L1_xattn_kv_w, L1_xattn_kv_b, L1_xattn_out_w, L1_xattn_out_b, L1_xattn_postnorm_w, L1_xattn_mlp_w1, L1_xattn_mlp_b1, L1_xattn_mlp_w2, L1_xattn_mlp_b2)
    return x

_drawn_inputs = setup_inputs


def setup_inputs(seed=0):
    import zlib

    import numpy as np

    out = dict(_drawn_inputs(seed))
    spreads = {'L0_xattn_ln1_w': (1.0, 0.2),
     'L0_xattn_ln1_b': (0.0, 0.1),
     'L0_xattn_ln2_w': (1.0, 0.6),
     'L0_xattn_ln2_b': (0.0, 0.8),
     'L0_xattn_gn_w': (1.0, 0.6),
     'L0_xattn_gn_b': (0.0, 0.8),
     'L1_xattn_q_b': (0.0, 0.8),
     'L1_xattn_kv_b': (0.0, 0.772),
     'L1_xattn_out_b': (0.0, 1.518),
     'L1_xattn_postnorm_w': (1.0, 0.2),
     'L1_xattn_mlp_b1': (0.0, 0.1),
     'L1_xattn_mlp_b2': (0.0, 0.1)}
    factors = {'ctx_2048': 6.475,
     'L0_xattn_maa_x': 6.497,
     'L0_xattn_maa_w': 8.0,
     'L0_xattn_maa_w1': 3.409,
     'L0_xattn_maa_w2': 3.443,
     'L0_xattn_decay_w1': 8.0,
     'L0_xattn_decay_w2': 8.0,
     'L0_xattn_faaaa': 3.702,
     'L0_xattn_fmaa_r': 8.0,
     'L0_xattn_fWr': 7.552,
     'L1_xattn_q_w': 8.0,
     'L1_xattn_kv_w': 8.0,
     'L1_xattn_out_w': 5.259}
    for name, (base, spread) in spreads.items():
        noise = np.random.default_rng([zlib.crc32(name.encode()), seed]).standard_normal(out[name].shape)
        drawn = base * np.exp(spread * noise) if base else spread * noise
        out[name] = jnp.asarray(drawn.astype(out[name].dtype))
    for name, factor in factors.items():
        out[name] = (out[name] * factor).astype(out[name].dtype)
    return out
```

```python
from contextlib import ExitStack

import concourse.bass as bass
from concourse import mybir

F32 = mybir.dt.float32
I32 = mybir.dt.int32
ALU = mybir.AluOpType
ACT = mybir.ActivationFunctionType
AX = mybir.AxisListType

P = 128
B, T, C = 8, 112, 512
NT = C // P
H, S = 32, 16
HT = P // S
NCTX = 375
NKEY = NCTX + T
KT_ROWS = 125
NKT = 4
NH, DH = 16, 32
HG = P // DH
FF = 4 * C
NF = FF // P
DM, DD, NMIX = 32, 64, 5
BC = 4
EPS_LN, EPS_RMS = 1e-5, 1e-6
MASKED = -1e30

MIX_V, MIX_K, MIX_W, MIX_R, MIX_G = range(NMIX)
VECS = ["ln1_w", "ln1_b", "ln2_w", "ln2_b", "maa_x", "faaaa", "gn_w", "gn_b", "fmaa_k", "fmaa_r",
        "q_b", "k_b", "v_b", "post_w"]
BIG = ["Wv", "Wk", "Wr", "Wg", "Wo", "fWk", "fWr", "fWv", "kw", "vw", "qw", "ow"]


def build(nc, a, out):
    with ExitStack() as ctx:
        def sb(name, shape, dt=F32):
            return ctx.enter_context(nc.sbuf_tensor(name, shape, dt))

        def sem(name):
            return ctx.enter_context(nc.semaphore(name))

        def dram(name, shape):
            return nc.dram_tensor(name, shape, F32, kind="Internal").ap()

        v_scratch = dram("v_scratch", (B, C, T))
        lat_scratch = dram("lat_scratch", (B, T, C))
        h1_scratch = dram("h1_scratch", (P, B, NT, T))

        wbig = sb("wbig", [P, len(BIG), NT, C])
        W = {n: wbig[:, i] for i, n in enumerate(BIG)}
        maa1 = sb("maa1", [P, NT, NMIX * DM])
        maa2 = sb("maa2", [DM + 1, NMIX, C])
        dec1 = sb("dec1", [P, NT, DD])
        dec2 = sb("dec2", [DD + 1, C])
        vec = sb("vec", [P, len(VECS), NT])
        V = {n: vec[:, i] for i, n in enumerate(VECS)}
        shifts = sb("shifts", [P, B, 2, NT])
        s0 = sb("s0", [P, NT, B, S])
        ob_rows = sb("ob_rows", [T, C])
        ident = sb("ident", [P, P])
        headsel = sb("headsel", [P, HT])
        neghalf = sb("neghalf", [P, H])
        x_in = sb("x_in", [T, C])
        x_res = sb("x_res", [T, C])
        rows = sb("rows", [T, C])
        stats = sb("stats", [T, 6])
        mv = sb("mv", [T, 2])
        small = sb("small", [T, 4])
        waiter = sb("waiter", [T, NH + 2])
        one = sb("one", [T, 1])
        xa = sb("xa", [P, NT, T + 1])
        sx = sb("sx", [P, NT, T])
        xxx = sb("xxx", [P, NT, T])
        t5 = sb("t5", [DM + 1, NMIX, T])
        tmp = sb("tmp", [P, 2, NT, T])
        xj = sb("xj", [P, 3, NT, T])
        dt65 = sb("dt65", [DD + 1, T])
        ws = sb("ws", [P, NT, T])
        ks = sb("ks", [P, NT, T])
        vt = sb("vt", [P, NT, T + 1])
        rt = sb("rt", [P, NT, T])
        gt = sb("gt", [P, NT, T])
        th = sb("th", [P, NT, T])
        ruk = sb("ruk", [P, NT, T])
        rk = sb("rk", [T, H])
        SCAN, CTX, KEYS = 2 * S * T, NT * NCTX, NT * NKEY
        region = sb("region", [P, SCAN + CTX + KEYS + NKT * C])
        work = region[:, 0:SCAN]
        scan = [work[:, i * S * T:(i + 1) * S * T].rearrange("p (a t) -> p a t", a=S) for i in range(2)]
        sm = [work[0:T, i * 488:i * 488 + NKEY] for i in range(4)]
        pts = [work[:, 4 * 488 + i * NKT * T:4 * 488 + (i + 1) * NKT * T].rearrange("p (k t) -> p k t", k=NKT)
               for i in range(3)]
        y = sb("y", [T, C])
        ysq = sb("ysq", [T, C])
        hs = sb("hs", [T, 4, H])
        x2 = sb("x2", [T, C])
        xc = sb("xc", [P, NT, T + 1])
        lat = sb("lat", [T, C])
        lat_ob = sb("lat_ob", [T, C])
        lt = sb("lt", [P, NT, T])
        qt = sb("qt", [P, NT, T])
        ctxt = region[:, SCAN:SCAN + CTX].rearrange("p (k n) -> p k n", k=NT)
        kt = region[:, SCAN + CTX:SCAN + CTX + KEYS].rearrange("p (k n) -> p k n", k=NT)
        vv = region[:, SCAN + CTX + KEYS:].rearrange("p (k n) -> p k n", k=NKT)
        mask_i = sb("mask_i", [T, NCTX], I32)
        mask_b = sb("mask_b", [T, NKEY])
        nmax = sb("nmax", [T, NH])
        rsum = sb("rsum", [T, 2, NH])
        flat = wbig[:, :, :, :].rearrange("p a k n -> p (a k n)")
        w1 = flat[:, 0:NT * FF].rearrange("p (k n) -> p k n", k=NT)
        w2 = flat[:, NT * FF:2 * NT * FF].rearrange("p (k n) -> p k n", k=NF)
        at = 2 * NT * FF
        h1 = flat[:, at:at + B * NT * T].rearrange("p (b k t) -> p b k t", b=B, k=NT)
        b1v = xxx[:, 0, 0:NF]
        b2_rows = ob_rows
        lat_all = flat[0:T, at + B * NT * T:at + B * NT * T + BC * C].rearrange("p (b n) -> p b n", b=BC)
        hid_all = region[:, 0:NF * BC * T].rearrange("p (f t) -> p f t", f=NF)

        banks = [ctx.enter_context(nc.psum_tensor(f"bank{i}", [P, 512], F32)) for i in (0,)]
        bB = ctx.enter_context(nc.psum_tensor("bankBC", [P, 1024], F32))
        rest = [ctx.enter_context(nc.psum_tensor(f"bank{i}", [P, 512], F32)) for i in range(3, 8)]
        bA = banks[0]
        bC = bB[:, 512:1024]
        bD, bE, bF, bG, bH = rest

        def hidden(f):
            return hid_all[:, f, :]

        def tiles(bank):
            return bank[:, 0:NT * T].rearrange("p (k t) -> p k t", k=NT)

        names = """const_loaded weights_loaded wlate_loaded xin_loaded xin_copied xn_ready xnT_ready xa_ready sx_ready
            xxx_ready tp_ready t_ready m_ready mix_ready xj_ready pv_ready pk_ready pr_ready pg_ready vt_ready
            ks_ready rt_ready th_ready gz_ready v_stored vb_loaded0 vb_loaded1 kvw_loaded a_ready s_ready prod_ready yacc_ready
            d1_ready dt_ready d2_ready w_exp ws_ready vtok_ready ruk_ready rkp_ready rk_ready y1_ready y_ready
            gsum gmean gcen gsq gvar gve grstd yn_ready ynT_ready ya_ready yg_ready wo_ready x2_ready
            st2 mv2 ve2 rstd2 x2n_ready xcT_ready xc_ready sxc_ready xk_ready kkp_ready rrp_ready kk_relu kk_ready
            ffn_ready rrt_ready ffg lat_ready latT_ready lt_ready latob_ready qp_ready qt_ready kl_ready ktl_ready
            vl_ready vvl_ready ctx_loaded kc_ready ktc_ready vc_ready vvc_ready mask_loaded mask_ready mask_eq
            s_done masked probs pt_ready pt_dve pt_act pvh on_ready rinv onT_ready ao_ready op_ready x1_ready turns
            ssq ve3 rstd3 x1n_ready h1_ready h1_stored lat_stored st1 mv1 ve1 rstd1 init_pool init_dve
            mlp_loaded lat_back0 lat_back1 lat_back2 lat_back3 hp_ready hid_ready mo_ready y2_ready out_stored0 out_stored1 out_stored2 out_stored3 s0_put h1_back w2_loaded memz""".split()
        s = {n: sem(n) for n in names}

        block = ctx.enter_context(nc.Block())

        @block.sync
        def _(sp):
            sp.dma_start(x_in[:, :], a["x"][0]).then_inc(s["xin_loaded"], 16)
            for dst, src in ((vec, "vec"), (shifts, "shifts"), (maa1, "maa1"), (maa2, "maa2"), (dec1, "dec1"),
                             (dec2, "dec2"), (s0, "s0")):
                sp.dma_start(dst[:], a[src]).then_inc(s["const_loaded"], 16)
            sp.dma_start(wbig[:, 0:4], a["wbig"][:, 0:4]).then_inc(s["weights_loaded"], 16)
            sp.dma_start(ctxt[:, :, :], a["ctxt"][0]).then_inc(s["ctx_loaded"], 16)
            sp.dma_start(wbig[:, 8:10], a["wbig"][:, 8:10]).then_inc(s["kvw_loaded"], 16)
            sp.dma_start(mask_i[:, :], a["mask"][0:1, :].broadcast_to([T, NCTX])).then_inc(s["mask_loaded"], 16)
            sp.dma_start(wbig[:, 4:8], a["wbig"][:, 4:8]).then_inc(s["wlate_loaded"], 16)
            sp.dma_start(wbig[:, 10:12], a["wbig"][:, 10:12]).then_inc(s["wlate_loaded"], 16)
            sp.dma_start(ob_rows[:, :], a["out_b"].broadcast_to([T, C])).then_inc(s["wlate_loaded"], 16)
            with sp.Fori(0, B) as b:
                sp.wait_ge(s["vt_ready"], b + 1)
                sp.dma_start(v_scratch[bass.ds(b, 1)].rearrange("b (k p) t -> p (b k) t", p=P),
                             vt[:, :, 0:T]).then_inc(s["v_stored"], 16)
                sp.wait_ge(s["v_stored"], b * 16 + 16)
                for c in range(NT):
                    if c < 2:
                        sp.wait_ge(s["turns"], b + 1)
                    else:
                        sp.wait_ge(s["yacc_ready"], b * NT + c - 1)
                    src = v_scratch[bass.ds(b, 1), c * P:(c + 1) * P, :].rearrange("b (h a) t -> (b h) a t", a=S)
                    sp.dma_start(scan[c % 2].rearrange("p a t -> p (a t)"),
                                 src.rearrange("h a t -> h (a t)").unsqueeze(1).broadcast_to([HT, S, S * T])
                                 ).then_inc(s[f"vb_loaded{c % 2}"], 16)
                nxt = sp.snap((b + 1) % B)
                sp.wait_ge(s["xin_copied"], b + 1)
                sp.wait_ge(s["xn_ready"], b + 1)
                sp.dma_start(x_in[:, :], a["x"][bass.ds(nxt, 1)].rearrange("b t c -> (b t) c")
                             ).then_inc(s["xin_loaded"], 16)
                sp.wait_ge(s["vc_ready"], 3 * b + 3)
                sp.dma_start(ctxt[:, :, :], a["ctxt"][bass.ds(nxt, 1)].rearrange("b p k n -> (b p) k n")
                             ).then_inc(s["ctx_loaded"], 16)
                sp.wait_ge(s["lat_ready"], b + 1)
                sp.dma_start(lat_scratch[bass.ds(b, 1)].rearrange("b t c -> (b t) c"), lat[:, :]
                             ).then_inc(s["lat_stored"], 16)
                sp.wait_ge(s["h1_ready"], b + 1)
                sp.dma_start(h1_scratch[:, bass.ds(b, 1)].rearrange("p b k t -> p (b k) t"), qt[:, :, :]
                             ).then_inc(s["h1_stored"], 16)
                sp.wait_ge(s["lat_stored"], b * 16 + 16)
                sp.wait_ge(s["h1_stored"], b * 16 + 16)
                sp.wait_ge(s["mask_eq"], b + 1)
                sp.dma_start(mask_i[:, :], a["mask"][bass.ds(nxt, 1), :].broadcast_to([T, NCTX])
                             ).then_inc(s["mask_loaded"], 16)
            sp.wait_ge(s["turns"], B + 1)
            sp.dma_start(w1, a["w1"]).then_inc(s["mlp_loaded"], 16)
            sp.dma_start(b1v, a["b1"]).then_inc(s["mlp_loaded"], 16)
            sp.wait_ge(s["h1_stored"], 16 * B)
            sp.dma_start(h1, h1_scratch).then_inc(s["mlp_loaded"], 16)
            sp.dma_start(w2, a["w2"]).then_inc(s["w2_loaded"], 16)
            sp.wait_ge(s["latob_ready"], B)
            sp.wait_ge(s["lat_stored"], 16 * B)
            sp.dma_start(b2_rows[:, :], a["b2"].broadcast_to([T, C])).then_inc(s["w2_loaded"], 16)
            for b in range(B):
                buf = lat_all[:, b % BC, :]
                if b >= BC:
                    sp.wait_ge(s[f"out_stored{b % BC}"], 16)
                sp.dma_start(buf, lat_scratch[b]).then_inc(s[f"lat_back{b % BC}"], 16)
            for b in range(BC):
                sp.wait_ge(s[f"out_stored{b}"], 16 * B // BC)

        @block.gpsimd
        def _(pool):
            g = nc.gpsimd
            g.memset(ident[:, :], 0.0).then_inc(s["init_pool"], 1)
            g.memset(headsel[:, :], 1.0).then_inc(s["init_pool"], 1)
            g.memset(neghalf[:, :], -0.5).then_inc(s["init_pool"], 1)
            g.memset(ws[:, :, 0:1], 0.0).then_inc(s["init_pool"], 1)
            g.memset(ks[:, :, 0:1], 0.0).then_inc(s["init_pool"], 1)
            g.memset(one[:, :], 1.0).then_inc(s["init_pool"], 1)
            g.memset(vt[:, :, 0:1], 0.0).then_inc(s["init_pool"], 1)
            pool.wait_ge(s["init_pool"], 7)
            g.affine_select(out=ident[:, :], in_=ident[:, :], compare_op=ALU.not_equal, fill=1.0, base=0,
                            pattern=[[-1, P]], channel_multiplier=1).then_inc(s["init_pool"], 1)
            g.affine_select(out=headsel[:, :], in_=headsel[:, :], compare_op=ALU.is_ge, fill=0.0, base=0,
                            pattern=[[-S, HT]], channel_multiplier=1).then_inc(s["init_pool"], 1)
            pool.wait_ge(s["init_pool"], 9)
            g.affine_select(out=headsel[:, :], in_=headsel[:, :], compare_op=ALU.is_ge, fill=0.0, base=S - 1,
                            pattern=[[S, HT]], channel_multiplier=-1).then_inc(s["init_pool"], 1)
            pool.wait_ge(s["init_pool"], 10)
            with pool.Fori(0, B) as b:
                pool.wait_ge(s["xin_loaded"], 16 * b + 16)
                pool.wait_ge(s["turns"], b + 1)
                g.tensor_tensor(x_res[:, :], x_in[:, :], one[:, :].broadcast_to([T, C]), ALU.mult).then_inc(s["xin_copied"], 1)
                pool.wait_ge(s["ve1"], b + 1)
                g.tensor_tensor(small[:, 1:2], small[:, 0:1], neghalf[0:T, 0:1], ALU.pow).then_inc(s["rstd1"], 1)
                for j in range(NMIX):
                    pool.wait_ge(s["mix_ready"], b * NMIX + j + 1)
                    if j >= 3:
                        pool.wait_ge(s[("pv_ready", "pk_ready")[j - 3]], b + 1)
                    g.tensor_tensor(xj[:, j % 3], tmp[:, j % 2], xa[:, :, 1:T + 1], ALU.add).then_inc(s["xj_ready"], 1)
                for c in range(NT):
                    buf = scan[c % 2]
                    pool.wait_ge(s[f"vb_loaded{c % 2}"], b * 32 + 16 * (c // 2) + 16)
                    pool.wait_ge(s["ks_ready"], b + 1)
                    g.tensor_tensor(buf, buf, ks[:, c:c + 1, :].broadcast_to([P, S, T]), ALU.mult
                                    ).then_inc(s["a_ready"], 1)
                    pool.wait_ge(s["a_ready"], b * NT + c + 1)
                    g.tensor_tensor(buf[:, :, 0:1], buf[:, :, 0:1],
                                    s0[:, c, bass.ds(b, 1), :].rearrange("p b a -> p a b"), ALU.add).then_inc(s["s0_put"], 1)
                pool.wait_ge(s["gve"], b + 1)
                g.tensor_tensor(hs[:, 3, :], hs[:, 2, :], neghalf[0:T, :], ALU.pow).then_inc(s["grstd"], 1)
                pool.wait_ge(s["ve2"], b + 1)
                g.tensor_tensor(small[:, 1:2], small[:, 0:1], neghalf[0:T, 0:1], ALU.pow).then_inc(s["rstd2"], 1)
                pool.wait_ge(s["lat_ready"], b + 1)
                pool.wait_ge(s["wlate_loaded"], 48)
                g.tensor_tensor(lat_ob[:, :], lat[:, :], ob_rows[:, :], ALU.add).then_inc(s["latob_ready"], 1)
                pool.wait_ge(s["ve3"], b + 1)
                g.tensor_tensor(small[:, 1:2], small[:, 0:1], neghalf[0:T, 0:1], ALU.pow).then_inc(s["rstd3"], 1)
            pool.wait_ge(s["w2_loaded"], 32)
            for b in range(B):
                pool.wait_ge(s[f"lat_back{b % BC}"], 16 * (b // BC + 1))
                g.tensor_tensor(lat_all[:, b % BC, :], lat_all[:, b % BC, :], b2_rows[:, :], ALU.add
                                ).then_inc(s["memz"], 1)

        @block.vector
        def _(dve):
            v = nc.vector
            v.memset(bE[:, :], 0.0).then_inc(s["init_dve"], 1)
            v.memset(bF[:, :], 0.0).then_inc(s["init_dve"], 1)
            v.memset(bG[:, :], 0.0).then_inc(s["init_dve"], 1)
            v.memset(t5[DM:DM + 1, :, :], 1.0).then_inc(s["init_dve"], 1)
            v.memset(dt65[DD:DD + 1, :], 1.0).then_inc(s["init_dve"], 1)
            v.memset(mask_b[:, NCTX:NKEY], 0.0).then_inc(s["init_dve"], 1)
            dve.wait_ge(s["init_dve"], 6)
            dve.wait_ge(s["const_loaded"], 16 * 7)
            dve.wait_ge(s["init_pool"], 10)
            with dve.Fori(0, B) as b:
                b1 = dve.snap(b + 1)
                dve.wait_ge(s["xin_loaded"], 16 * b + 16)
                v.bn_stats(stats[:, :], x_in[:, :]).then_inc(s["st1"], 1)
                dve.wait_ge(s["st1"], b1)
                v.memset(waiter[:, 0:1], 0.0)
                v.bn_aggr(mv[:, :], stats[:, :]).then_inc(s["mv1"], 1)
                dve.wait_ge(s["mv1"], b1)
                v.tensor_scalar(small[:, 0:1], mv[:, 1:2], EPS_LN, None, ALU.add).then_inc(s["ve1"], 1)
                dve.wait_ge(s["turns"], b1)
                dve.wait_ge(s["rstd1"], b1)
                v.tensor_scalar(rows[:, :], x_in[:, :], mv[:, 0:1], small[:, 1:2], ALU.subtract, ALU.mult
                                ).then_inc(s["xn_ready"], 1)
                dve.wait_ge(s["xa_ready"], b1)
                v.tensor_tensor(sx[:, :, :], xa[:, :, 0:T], xa[:, :, 1:T + 1], ALU.subtract).then_inc(s["sx_ready"], 1)
                dve.wait_ge(s["sx_ready"], b1)
                for k in range(NT):
                    i = v.scalar_tensor_tensor(out=xxx[:, k, :], in0=sx[:, k, :], scalar=V["maa_x"][:, k:k + 1],
                                               in1=xa[:, k, 1:T + 1], op0=ALU.mult, op1=ALU.add)
                i.then_inc(s["xxx_ready"], 1)
                for j in range(NMIX):
                    dve.wait_ge(s["m_ready"], b * NMIX + j + 1)
                    if j >= 2:
                        dve.wait_ge(s["xj_ready"], b * NMIX + j - 1)
                    v.tensor_tensor(tmp[:, j % 2], tiles((bD, bE)[j % 2]), sx[:, :, :], ALU.mult
                                    ).then_inc(s["mix_ready"], 1)
                dve.wait_ge(s["pk_ready"], b1)
                v.tensor_copy(ks[:, :, 1:T], tiles(bB)[:, :, 0:T - 1]).then_inc(s["ks_ready"], 1)
                dve.wait_ge(s["rt_ready"], b1)
                for k in range(NT):
                    i = v.scalar_tensor_tensor(out=ruk[:, k, :], in0=tiles(bB)[:, k, :], scalar=V["faaaa"][:, k:k + 1],
                                               in1=rt[:, k, :], op0=ALU.mult, op1=ALU.mult)
                i.then_inc(s["ruk_ready"], 1)
                for c in range(NT):
                    buf = scan[c % 2]
                    one = buf.rearrange("p a t -> p (a t)")
                    dve.wait_ge(s["s0_put"], b * NT + c + 1)
                    dve.wait_ge(s["ws_ready"], b1)
                    for q in range(S):
                        i = v.tensor_tensor_scan(buf[:, q, :], ws[:, c, :], buf[:, q, :], 0.0, ALU.mult, ALU.add)
                    i.then_inc(s["s_ready"], 1)
                    dve.wait_ge(s["s_ready"], b * NT + c + 1)
                    v.tensor_tensor(buf, buf, rt[:, c:c + 1, :].broadcast_to([P, S, T]), ALU.mult
                                    ).then_inc(s["prod_ready"], 1)
                    if c == 0:
                        dve.wait_ge(s["th_ready"], b1)
                        v.scalar_tensor_tensor(out=gt[:, :, :], in0=th[:, :, :], scalar=1.0, in1=tiles(bG),
                                               op0=ALU.add, op1=ALU.mult).then_inc(s["gz_ready"], 1)
                        dve.wait_ge(s["rkp_ready"], b1)
                        v.tensor_copy(rk[:, :], bF[0:T, 0:H]).then_inc(s["rk_ready"], 1)
                        dve.wait_ge(s["rk_ready"], b1)
                        dve.wait_ge(s["vtok_ready"], b1)
                        v.tensor_tensor(y[:, :].rearrange("p (h a) -> p h a", a=S),
                                        bH[0:T, :].rearrange("p (h a) -> p h a", a=S),
                                        rk[:, :].unsqueeze(2).broadcast_to([T, H, S]), ALU.mult
                                        ).then_inc(s["y1_ready"], 1)
                yh = y[:, :].rearrange("p (h a) -> p h a", a=S)
                sqh = ysq[:, :].rearrange("p (h a) -> p h a", a=S)

                def per_head(ap):
                    return ap.unsqueeze(2).broadcast_to([T, H, S])
                dve.wait_ge(s["yacc_ready"], b * NT + NT)
                dve.wait_ge(s["y1_ready"], b1)
                v.tensor_tensor(y[:, :], y[:, :], bC[0:T, :], ALU.add).then_inc(s["y_ready"], 1)
                dve.wait_ge(s["y_ready"], b1)
                v.tensor_reduce(hs[:, 0, :], yh, AX.X, ALU.add).then_inc(s["gsum"], 1)
                dve.wait_ge(s["gsum"], b1)
                v.tensor_scalar(hs[:, 1, :], hs[:, 0, :], 1.0 / S, None, ALU.mult).then_inc(s["gmean"], 1)
                dve.wait_ge(s["gmean"], b1)
                v.tensor_tensor(yh, yh, per_head(hs[:, 1, :]), ALU.subtract).then_inc(s["gcen"], 1)
                dve.wait_ge(s["gcen"], b1)
                v.tensor_tensor(sqh, yh, yh, ALU.mult).then_inc(s["gsq"], 1)
                dve.wait_ge(s["gsq"], b1)
                v.tensor_reduce(hs[:, 0, :], sqh, AX.X, ALU.add).then_inc(s["gvar"], 1)
                dve.wait_ge(s["gvar"], b1)
                v.tensor_scalar(hs[:, 2, :], hs[:, 0, :], 1.0 / S, EPS_LN, ALU.mult, ALU.add).then_inc(s["gve"], 1)
                dve.wait_ge(s["grstd"], b1)
                v.tensor_tensor(rows[:, :].rearrange("p (h a) -> p h a", a=S), yh, per_head(hs[:, 3, :]), ALU.mult
                                ).then_inc(s["yn_ready"], 1)
                dve.wait_ge(s["ya_ready"], b1)
                v.scalar_tensor_tensor(out=th[:, :, :], in0=th[:, :, :], scalar=0.5, in1=gt[:, :, :],
                                       op0=ALU.mult, op1=ALU.mult).then_inc(s["yg_ready"], 1)
                dve.wait_ge(s["wo_ready"], b1)
                v.tensor_tensor(x2[:, :], x_res[:, :], bH[0:T, :], ALU.add).then_inc(s["x2_ready"], 1)
                dve.wait_ge(s["x2_ready"], b1)
                v.bn_stats(stats[:, :], x2[:, :]).then_inc(s["st2"], 1)
                dve.wait_ge(s["st2"], b1)
                v.memset(waiter[:, 1:2], 0.0)
                v.bn_aggr(mv[:, :], stats[:, :]).then_inc(s["mv2"], 1)
                dve.wait_ge(s["mv2"], b1)
                v.tensor_scalar(small[:, 0:1], mv[:, 1:2], EPS_LN, None, ALU.add).then_inc(s["ve2"], 1)
                dve.wait_ge(s["rstd2"], b1)
                v.tensor_scalar(rows[:, :], x2[:, :], mv[:, 0:1], small[:, 1:2], ALU.subtract, ALU.mult
                                ).then_inc(s["x2n_ready"], 1)
                dve.wait_ge(s["xc_ready"], b1)
                v.tensor_tensor(sx[:, :, :], xc[:, :, 0:T], xc[:, :, 1:T + 1], ALU.subtract).then_inc(s["sxc_ready"], 1)
                dve.wait_ge(s["sxc_ready"], b1)
                for m, w in enumerate(("fmaa_k", "fmaa_r")):
                    for k in range(NT):
                        i = v.scalar_tensor_tensor(out=xj[:, m, k, :], in0=sx[:, k, :], scalar=V[w][:, k:k + 1],
                                                   in1=xc[:, k, 1:T + 1], op0=ALU.mult, op1=ALU.add)
                    i.then_inc(s["xk_ready"], 1)
                dve.wait_ge(s["kk_relu"], b1)
                v.tensor_tensor(ruk[:, :, :], tmp[:, 0], tmp[:, 0], ALU.mult).then_inc(s["kk_ready"], 1)
                dve.wait_ge(s["rrt_ready"], b1)
                dve.wait_ge(s["ffn_ready"], b1)
                v.scalar_tensor_tensor(out=y[:, :], in0=ysq[:, :], scalar=1.0, in1=bE[0:T, :], op0=ALU.add,
                                       op1=ALU.mult).then_inc(s["ffg"], 1)
                dve.wait_ge(s["ffg"], b1)
                v.scalar_tensor_tensor(out=lat[:, :], in0=y[:, :], scalar=0.5, in1=x2[:, :], op0=ALU.mult,
                                       op1=ALU.add).then_inc(s["lat_ready"], 1)
                dve.wait_ge(s["mask_loaded"], 16 * b + 16)
                v.tensor_scalar(mask_b[:, 0:NCTX], mask_i[:, :], 0.0, MASKED, ALU.is_equal, ALU.mult
                                ).then_inc(s["mask_eq"], 1)
                dve.wait_ge(s["mask_eq"], b1)
                for h in range(NH + 2):
                    if h < NH:
                        dve.wait_ge(s["s_done"], b * NH + h + 1)
                        if h >= 4:
                            dve.wait_ge(s["pt_ready"], b * NH + h - 3)
                        v.memset(waiter[:, h + 2:h + 3], 0.0)
                        v.tensor_tensor_reduce(sm[h % 4], (bA, bB, bD)[h % 3][0:T, 0:NKEY], mask_b[:, :],
                                               -1.0 / DH, 3e38, ALU.add, ALU.min, nmax[:, h:h + 1]
                                               ).then_inc(s["masked"], 1)
                    if h >= 2 and h % 2 == 0:
                        g = h - 2
                        dve.wait_ge(s["pt_ready"], b * NH + g + 1)
                        if g >= 3:
                            dve.wait_ge(s["pvh"], b * NH + g - 2)
                        v.tensor_copy(pts[g % 3][0:KT_ROWS], tiles((bE, bF, bG)[g % 3])[0:KT_ROWS]
                                      ).then_inc(s["pt_dve"], 1)
                dve.wait_ge(s["probs"], b * NH + NH)
                v.reciprocal(rsum[:, 1, :], rsum[:, 0, :]).then_inc(s["rinv"], 1)
                dve.wait_ge(s["rinv"], b1)
                dve.wait_ge(s["pvh"], b * NH + NH)
                v.tensor_tensor(rows[:, :].rearrange("p (h d) -> p h d", d=DH),
                                bH[0:T, :].rearrange("p (h d) -> p h d", d=DH),
                                rsum[:, 1, :].unsqueeze(2).broadcast_to([T, NH, DH]), ALU.mult
                                ).then_inc(s["on_ready"], 1)
                dve.wait_ge(s["op_ready"], b1)
                dve.wait_ge(s["latob_ready"], b1)
                v.tensor_tensor(x2[:, :], bA[0:T, :], lat_ob[:, :], ALU.add).then_inc(s["x1_ready"], 1)
                dve.wait_ge(s["x1_ready"], b1)
                v.tensor_tensor_reduce(ysq[:, :], x2[:, :], x2[:, :], 1.0 / C, EPS_RMS, ALU.mult, ALU.add,
                                       small[:, 0:1]).then_inc(s["ve3"], 1)
                dve.wait_ge(s["rstd3"], b1)
                v.tensor_scalar(rows[:, :], x2[:, :], small[:, 1:2], None, ALU.mult).then_inc(s["x1n_ready"], 1)
            for b in range(B):
                dve.wait_ge(s["mo_ready"], b + 1)
                dve.wait_ge(s["memz"], b + 1)
                buf = lat_all[:, b % BC, :]
                v.tensor_tensor(buf, (bE, bF)[b % 2][0:T, :], buf, ALU.add).then_inc(s["y2_ready"], 1)

        @block.scalar
        def _(act):
            c_ = nc.scalar
            act.wait_ge(s["const_loaded"], 16 * 7)

            def columns(dst, src, scale, bias, done):
                for k in range(NT):
                    kw = {"bias": V[bias][:, k:k + 1]}
                    if scale is not None:
                        kw["scale"] = V[scale][:, k:k + 1]
                    i = c_.activation(dst[:, k, :], src[:, k, :], ACT.Identity, **kw)
                i.then_inc(s[done], 1)

            with act.Fori(0, B) as b:
                b1 = act.snap(b + 1)
                act.wait_ge(s["turns"], b1)
                c_.copy(xa[:, :, 0:1], shifts[:, bass.ds(b, 1), 1, :].rearrange("p b k -> p k b"))
                c_.copy(xc[:, :, 0:1], shifts[:, bass.ds(b, 1), 0, :].rearrange("p b k -> p k b"))
                act.wait_ge(s["xnT_ready"], b1)
                columns(xa[:, :, 1:T + 1], tiles(bA), "ln1_w", "ln1_b", "xa_ready")
                act.wait_ge(s["tp_ready"], b1)
                c_.activation(t5[0:DM, :, :], bB[0:DM, 0:NMIX * P].rearrange("p (j t) -> p j t", t=P)[:, :, 0:T],
                              ACT.Tanh).then_inc(s["t_ready"], 1)
                act.wait_ge(s["pv_ready"], b1)
                c_.copy(vt[:, :, 1:T + 1], tiles(bA)).then_inc(s["vt_ready"], 1)
                act.wait_ge(s["d1_ready"], b1)
                c_.activation(dt65[0:DD, :], bF[0:DD, 0:T], ACT.Tanh).then_inc(s["dt_ready"], 1)
                act.wait_ge(s["d2_ready"], b1)
                c_.activation(th[:, :, :], tiles(bF), ACT.Exp).then_inc(s["w_exp"], 1)
                act.wait_ge(s["w_exp"], b1)
                c_.activation(ws[:, :, 1:T], th[:, :, 0:T - 1], ACT.Exp, scale=-1.0).then_inc(s["ws_ready"], 1)
                act.wait_ge(s["pr_ready"], b1)
                c_.copy(rt[:, :, :], tiles(bC)).then_inc(s["rt_ready"], 1)
                act.wait_ge(s["pg_ready"], b1)
                act.wait_ge(s["ws_ready"], b1)
                c_.activation(th[:, :, :], tiles(bG), ACT.Tanh, scale=0.5).then_inc(s["th_ready"], 1)
                for g in range(NT):
                    act.wait_ge(s["kc_ready"], b * NT + g + 1)
                    c_.activation(kt[:, g, 0:NCTX], (bA, bD)[g % 2][:, 0:NCTX], ACT.Identity,
                                  bias=V["k_b"][:, g:g + 1]).then_inc(s["ktc_ready"], 1)
                for j in range(3):
                    act.wait_ge(s["vc_ready"], b * 3 + j + 1)
                    c_.copy(vv[0:KT_ROWS, j, :], (bE, bD)[j % 2][0:KT_ROWS, :]).then_inc(s["vvc_ready"], 1)
                act.wait_ge(s["ynT_ready"], b1)
                act.wait_ge(s["gz_ready"], b1)
                columns(th, tiles(bG), "gn_w", "gn_b", "ya_ready")
                act.wait_ge(s["xcT_ready"], b1)
                columns(xc[:, :, 1:T + 1], tiles(bA), "ln2_w", "ln2_b", "xc_ready")
                act.wait_ge(s["kkp_ready"], b1)
                c_.activation(tmp[:, 0], tiles(bB), ACT.Relu).then_inc(s["kk_relu"], 1)
                act.wait_ge(s["rrp_ready"], b1)
                c_.activation(ysq[:, :], bD[0:T, :], ACT.Tanh, scale=0.5).then_inc(s["rrt_ready"], 1)
                act.wait_ge(s["latT_ready"], b1)
                c_.copy(lt[:, :, :], tiles(bF)).then_inc(s["lt_ready"], 1)
                act.wait_ge(s["qp_ready"], b1)
                columns(qt, tiles(bG), None, "q_b", "qt_ready")
                act.wait_ge(s["kl_ready"], b1)
                columns(kt[:, :, NCTX:NKEY], tiles(bH), None, "k_b", "ktl_ready")
                act.wait_ge(s["vl_ready"], b1)
                c_.copy(vv[0:T, 3, :], bC[0:T, :]).then_inc(s["vvl_ready"], 1)
                for h in range(NH + 2):
                    if h < NH:
                        act.wait_ge(s["masked"], b * NH + h + 1)
                        c_.activation(sm[h % 4], sm[h % 4], ACT.Exp, bias=nmax[:, h:h + 1], scale=-1.0,
                                      accum_out=rsum[:, 0, h:h + 1]).then_inc(s["probs"], 1)
                    if h >= 2 and h % 2 == 1:
                        g = h - 2
                        act.wait_ge(s["pt_ready"], b * NH + g + 1)
                        if g >= 3:
                            act.wait_ge(s["pvh"], b * NH + g - 2)
                        c_.copy(pts[g % 3][0:KT_ROWS], tiles((bE, bF, bG)[g % 3])[0:KT_ROWS]
                                ).then_inc(s["pt_act"], 1)
                act.wait_ge(s["onT_ready"], b1)
                columns(lt, tiles(bC), None, "v_b", "ao_ready")
                act.wait_ge(s["turns"], b + 2)
                for k in range(NT):
                    i = c_.activation(qt[:, k, :], tiles(bB)[:, k, :], ACT.Copy, scale=V["post_w"][:, k:k + 1])
                i.then_inc(s["h1_ready"], 1)
            act.wait_ge(s["mlp_loaded"], 48)
            for n in range(2):
                for f in range(NF):
                    act.wait_ge(s["hp_ready"], n * NF + f + 1)
                    if n:
                        act.wait_ge(s["mo_ready"], BC)
                    c_.activation(hidden(f), (bA, bD, bG, bH)[f % 4][:, 0:BC * T], ACT.Gelu_apprx_tanh,
                                  bias=b1v[:, f:f + 1]).then_inc(s["hid_ready"], 1)
            for b in range(B):
                act.wait_ge(s["y2_ready"], b + 1)
                act.dma_start(out[b], lat_all[:, b % BC, :]).then_inc(s[f"out_stored{b % BC}"], 16)

        @block.tensor
        def _(pe):
            t_ = nc.tensor

            def turn(dst, src, done):
                for k in range(NT):
                    i = t_.transpose(tiles(dst)[:, k, :], src[:, k * P:(k + 1) * P], ident[0:T, 0:T])
                i.then_inc(s[done], 1)

            def to_columns(dst, w, x, done):
                for m in range(NT):
                    for k in range(NT):
                        i = t_.matmul(tiles(dst)[:, m, :], w[:, k, m * P:(m + 1) * P], x[:, k, :],
                                      start=k == 0, stop=k == NT - 1)
                i.then_inc(s[done], 1)

            def to_rows(dst, w, x, done, m=T):
                for k in range(NT):
                    i = t_.matmul(dst[0:m, :], x[:, k, :], w[:, k, :], start=k == 0, stop=k == NT - 1)
                i.then_inc(s[done], 1)

            pe.wait_ge(s["init_pool"], 10)
            pe.wait_ge(s["init_dve"], 6)
            pe.wait_ge(s["const_loaded"], 16 * 7)
            pe.sem_inc(s["turns"], 1)
            with pe.Fori(0, B) as b:
                b1 = pe.snap(b + 1)
                pe.wait_ge(s["xn_ready"], b1)
                turn(bA, rows, "xnT_ready")
                pe.wait_ge(s["xxx_ready"], b1)
                for j in range(NMIX):
                    for k in range(NT):
                        i = t_.matmul(bB[0:DM, j * P:j * P + T], maa1[:, k, j * DM:(j + 1) * DM], xxx[:, k, :],
                                      start=k == 0, stop=k == NT - 1)
                i.then_inc(s["tp_ready"], 1)
                pe.wait_ge(s["t_ready"], b1)

                def adapter(j):
                    if j >= 2:
                        pe.wait_ge(s["mix_ready"], b * NMIX + j - 1)
                    for m in range(NT):
                        i = t_.matmul(tiles((bD, bE)[j % 2])[:, m, :], maa2[:, j, m * P:(m + 1) * P], t5[:, j, :],
                                      start=True, stop=True)
                    i.then_inc(s["m_ready"], 1)

                adapter(MIX_V)
                adapter(MIX_K)
                adapter(MIX_W)
                pe.wait_ge(s["weights_loaded"], 16)
                pe.wait_ge(s["xj_ready"], b * NMIX + MIX_V + 1)
                to_columns(bA, W["Wv"], xj[:, MIX_V % 3], "pv_ready")
                adapter(MIX_R)
                pe.wait_ge(s["xj_ready"], b * NMIX + MIX_K + 1)
                to_columns(bB, W["Wk"], xj[:, MIX_K % 3], "pk_ready")
                adapter(MIX_G)
                pe.wait_ge(s["xj_ready"], b * NMIX + MIX_W + 1)
                for k in range(NT):
                    i = t_.matmul(bF[0:DD, 0:T], dec1[:, k, :], xj[:, MIX_W % 3, k, :], start=k == 0, stop=k == NT - 1)
                i.then_inc(s["d1_ready"], 1)
                pe.wait_ge(s["xj_ready"], b * NMIX + MIX_R + 1)
                to_columns(bC, W["Wr"], xj[:, MIX_R % 3], "pr_ready")
                pe.wait_ge(s["dt_ready"], b1)
                for m in range(NT):
                    i = t_.matmul(tiles(bF)[:, m, :], dec2[:, m * P:(m + 1) * P], dt65[:, :], start=True, stop=True)
                i.then_inc(s["d2_ready"], 1)
                pe.wait_ge(s["xj_ready"], b * NMIX + MIX_G + 1)
                to_columns(bG, W["Wg"], xj[:, MIX_G % 3], "pg_ready")
                pe.wait_ge(s["vt_ready"], b1)
                for k in range(NT):
                    i = t_.transpose(bH[0:T, k * P:(k + 1) * P], vt[:, k, 1:T + 1], ident[:, :])
                i.then_inc(s["vtok_ready"], 1)
                pe.wait_ge(s["ctx_loaded"], 16 * b + 16)
                pe.wait_ge(s["kvw_loaded"], 16)
                for g in range(NT):
                    if g == 1:
                        pe.wait_ge(s["mix_ready"], b * NMIX + NMIX)
                    if g >= 2:
                        pe.wait_ge(s["ktc_ready"], b * NT + g - 1)
                    for k in range(NT):
                        i = t_.matmul((bA, bD)[g % 2][:, 0:NCTX], W["kw"][:, k, g * P:(g + 1) * P], ctxt[:, k, :],
                                      start=k == 0, stop=k == NT - 1)
                    i.then_inc(s["kc_ready"], 1)
                pe.wait_ge(s["ruk_ready"], b1)
                pe.wait_ge(s["w_exp"], b1)
                for k in range(NT):
                    i = t_.matmul(bF[0:T, k * HT:(k + 1) * HT], ruk[:, k, :], headsel[:, :], start=True, stop=True)
                i.then_inc(s["rkp_ready"], 1)
                pe.wait_ge(s["rt_ready"], b1)
                for c in range(NT):
                    if c < 3:
                        if c == 1:
                            pe.wait_ge(s["ktc_ready"], b * NT + NT)
                        if c == 2:
                            pe.wait_ge(s["vvc_ready"], b * 3 + 1)
                        for k in range(NT):
                            i = t_.matmul((bE, bD)[c % 2][0:KT_ROWS, :], ctxt[:, k, c * KT_ROWS:(c + 1) * KT_ROWS],
                                          W["vw"][:, k, :], start=k == 0, stop=k == NT - 1)
                        i.then_inc(s["vc_ready"], 1)
                    pe.wait_ge(s["prod_ready"], b * NT + c + 1)
                    yc = bC[0:T, c * P:(c + 1) * P].rearrange("p (h a) -> p h a", a=S)
                    for q in range(S):
                        i = t_.matmul(yc[:, :, q], scan[c % 2][:, q, :], headsel[:, :], start=True, stop=True)
                    i.then_inc(s["yacc_ready"], 1)
                pe.wait_ge(s["yn_ready"], b1)
                pe.wait_ge(s["gz_ready"], b1)
                turn(bG, rows, "ynT_ready")
                pe.wait_ge(s["yg_ready"], b1)
                pe.wait_ge(s["wlate_loaded"], 48)
                pe.wait_ge(s["y1_ready"], b1)
                to_rows(bH, W["Wo"], th, "wo_ready")
                pe.wait_ge(s["x2n_ready"], b1)
                turn(bA, rows, "xcT_ready")
                pe.wait_ge(s["xk_ready"], 2 * b + 1)
                to_columns(bB, W["fWk"], xj[:, 0], "kkp_ready")
                pe.wait_ge(s["xk_ready"], 2 * b + 2)
                pe.wait_ge(s["vvc_ready"], b * 3 + 3)
                to_rows(bD, W["fWr"], xj[:, 1], "rrp_ready")
                pe.wait_ge(s["kk_ready"], b1)
                to_rows(bE, W["fWv"], ruk, "ffn_ready")
                pe.wait_ge(s["lat_ready"], b1)
                turn(bF, lat, "latT_ready")
                pe.wait_ge(s["lt_ready"], b1)
                to_columns(bG, W["qw"], lt, "qp_ready")
                to_columns(bH, W["kw"], lt, "kl_ready")
                to_rows(bC, W["vw"], lt, "vl_ready")
                pe.wait_ge(s["qt_ready"], b1)
                pe.wait_ge(s["ktl_ready"], b1)
                for h in range(NH + 3):
                    if h < NH:
                        g, r = h // HG, h % HG * DH
                        if h >= 3:
                            pe.wait_ge(s["masked"], b * NH + h - 2)
                        t_.matmul((bA, bB, bD)[h % 3][0:T, 0:NKEY], qt[r:r + DH, g, :], kt[r:r + DH, g, :],
                                  start=True, stop=True).then_inc(s["s_done"], 1)
                    if 2 <= h < NH + 2:
                        g = h - 2
                        pe.wait_ge(s["probs"], b * NH + g + 1)
                        if g >= 3:
                            pe.wait_ge(s["pt_dve" if (g - 3) % 2 == 0 else "pt_act"], b * (NH // 2) + (g - 3) // 2 + 1)
                        for j in range(NKT):
                            n = KT_ROWS if j < 3 else T
                            i = t_.transpose(tiles((bE, bF, bG)[g % 3])[0:n, j, :],
                                             sm[g % 4][:, j * KT_ROWS:j * KT_ROWS + n], ident[0:T, 0:T])
                        i.then_inc(s["pt_ready"], 1)
                    if h >= 3:
                        g = h - 3
                        pe.wait_ge(s["pt_dve" if g % 2 == 0 else "pt_act"], b * (NH // 2) + g // 2 + 1)
                        if g == 0:
                            pe.wait_ge(s["vvl_ready"], b1)
                        for j in range(NKT):
                            n = KT_ROWS if j < 3 else T
                            i = t_.matmul(bH[0:T, g * DH:(g + 1) * DH], pts[g % 3][0:n, j, :],
                                          vv[0:n, j, g * DH:(g + 1) * DH], start=j == 0, stop=j == NKT - 1)
                        i.then_inc(s["pvh"], 1)
                pe.wait_ge(s["on_ready"], b1)
                turn(bC, rows, "onT_ready")
                pe.wait_ge(s["ao_ready"], b1)
                to_rows(bA, W["ow"], lt, "op_ready")
                pe.wait_ge(s["x1n_ready"], b1)
                turn(bB, rows, "turns")
            pe.wait_ge(s["mlp_loaded"], 48)
            for n in range(2):
                for f in range(NF):
                    if n * NF + f >= 4:
                        pe.wait_ge(s["hid_ready"], n * NF + f - 3)
                    for k in range(NT):
                        rhs = h1[:, n * BC:(n + 1) * BC, k, :]
                        i = t_.matmul((bA, bD, bG, bH)[f % 4][:, 0:BC * T], w1[:, k, f * P:(f + 1) * P], rhs,
                                      start=k == 0, stop=k == NT - 1)
                    i.then_inc(s["hp_ready"], 1)
                pe.wait_ge(s["w2_loaded"], 32)
                for b in range(BC):
                    m = n * BC + b
                    if m >= 2:
                        pe.wait_ge(s["y2_ready"], m - 1)
                    for f in range(NF):
                        if b == 0:
                            pe.wait_ge(s["hid_ready"], n * NF + f + 1)
                        i = t_.matmul((bE, bF)[m % 2][0:T, :], hidden(f)[:, b * T:(b + 1) * T], w2[:, f, :],
                                      start=f == 0, stop=f == NF - 1)
                    i.then_inc(s["mo_ready"], 1)


def kernel(**inputs):
    import numpy as np
    import concourse.bacc as bacc
    from concourse.bass_utils import run_bass_kernel_spmd as run

    i = {k: np.asarray(v) for k, v in inputs.items()}
    L0 = {k[len("L0_xattn_"):]: v for k, v in i.items() if k.startswith("L0_xattn_")}
    L1 = {k[len("L1_xattn_"):]: v for k, v in i.items() if k.startswith("L1_xattn_")}

    def cols(v):
        return v.reshape(-1, P).T

    def wt(w):
        return w.reshape(-1, P, w.shape[1]).transpose(1, 0, 2)

    kv_w = L1["kv_w"].reshape(C, C, 2)
    kv_b = L1["kv_b"].reshape(C, 2)
    vecs = dict(ln1_w=L0["ln1_w"], ln1_b=L0["ln1_b"], ln2_w=L0["ln2_w"], ln2_b=L0["ln2_b"], maa_x=L0["maa_x"],
                faaaa=L0["faaaa"].reshape(C), gn_w=L0["gn_w"], gn_b=L0["gn_b"], fmaa_k=L0["fmaa_k"],
                fmaa_r=L0["fmaa_r"], q_b=L1["q_b"], k_b=kv_b[:, 0], v_b=kv_b[:, 1], post_w=L1["postnorm_w"])
    big = dict(Wv=L0["Wv"].T, Wk=L0["Wk"].T, Wr=L0["Wr"].T, Wg=L0["Wg"].T, Wo=L0["Wo"].T, fWk=L0["fWk"].T,
               fWr=L0["fWr"].T, fWv=L0["fWv"].T, kw=kv_w[:, :, 0], vw=kv_w[:, :, 1], qw=L1["q_w"], ow=L1["out_w"])
    order = [2, 1, 0, 3, 4]
    maa1 = L0["maa_w1"].reshape(C, NMIX, DM)[:, order].reshape(C, NMIX * DM)
    maa = [L0["maa_" + n] for n in "vkwrg"]
    c = i["ctx_2048"]
    arrays = dict(
        x=i["x"],
        vec=np.stack([cols(vecs[n]) for n in VECS], 1),
        shifts=c[:, 0:2].reshape(B, 2, NT, P).transpose(3, 0, 1, 2),
        s0=c[:, 2:2 + S].reshape(B, NT, P, S).transpose(2, 1, 0, 3),
        ctxt=c.reshape(B, NCTX, NT, P).transpose(0, 3, 2, 1),
        mask=i["mask_BxS2_ik0"],
        maa1=wt(maa1),
        maa2=np.concatenate([L0["maa_w2"][order].transpose(1, 0, 2), np.stack(maa)[None]], 0),
        dec1=wt(L0["decay_w1"]),
        dec2=np.concatenate([L0["decay_w2"], L0["time_decay"][None]], 0),
        wbig=np.stack([wt(big[n]) for n in BIG], 1),
        w1=wt(L1["mlp_w1"]), w2=wt(L1["mlp_w2"]), b1=cols(L1["mlp_b1"]),
        b2=L1["mlp_b2"][None], out_b=L1["out_b"][None],
    )
    nc = bacc.Bacc("TRN2", target_bir_lowering=False, num_devices=1)
    feed, aps = {}, {}
    for n, v in arrays.items():
        feed[f"in_{n}"] = np.ascontiguousarray(v)
        aps[n] = nc.dram_tensor(f"in_{n}", v.shape, mybir.dt.from_np(v.dtype), kind="ExternalInput").ap()
    out = nc.dram_tensor("out_0", (B, T, C), F32, kind="ExternalOutput").ap()
    build(nc, aps, out)
    r = run(nc, [feed], core_ids=[0])
    return r.results[0]["out_0"]
```

```python
from contextlib import ExitStack

import concourse.bass as bass
from concourse import mybir

F32 = mybir.dt.float32
I32 = mybir.dt.int32
ALU = mybir.AluOpType
ACT = mybir.ActivationFunctionType
AX = mybir.AxisListType

P = 128
B, T, C = 8, 112, 512
NT = C // P
H, S = 32, 16
HT = P // S
NCTX = 375
NKEY = NCTX + T
KT_ROWS = 125
NKT = 4
NH, DH = 16, 32
HG = P // DH
FF = 4 * C
NF = FF // P
DM, DD, NMIX = 32, 64, 5
VS = 8
NCH = NT * S // VS
NBUF = 4
BC = 4
EPS_LN, EPS_RMS = 1e-5, 1e-6
MASKED = -1e30

MIX_V, MIX_K, MIX_W, MIX_R, MIX_G = range(NMIX)
MIX_BANK = (7, 5, 6, 5, 7)
CTX_BANK = (3, 2, 3, 2, 3, 2, 3)
VECS = ["ln1_w", "ln1_b", "ln2_w", "ln2_b", "maa_x", "faaaa", "gn_w", "gn_b", "fmaa_k", "fmaa_r",
        "q_b", "k_b", "v_b", "post_w", "maa_v", "maa_k", "maa_w", "maa_r", "maa_g"]
BIG = ["Wv", "Wk", "Wr", "Wg", "Wo", "fWk", "fWr", "fWv", "kw", "vw", "qw", "ow"]


def build(nc, a, out):
    with ExitStack() as ctx:
        def sb(name, shape, dt=F32):
            return ctx.enter_context(nc.sbuf_tensor(name, shape, dt))

        def sem(name):
            return ctx.enter_context(nc.semaphore(name))

        def dram(name, shape):
            return nc.dram_tensor(name, shape, F32, kind="Internal").ap()

        v_scratch = dram("v_scratch", (B, C, T))
        lat_scratch = dram("lat_scratch", (B, T, C))
        h1_scratch = dram("h1_scratch", (P, B, NT, T))

        wbig = sb("wbig", [P, len(BIG), NT, C])
        W = {n: wbig[:, i] for i, n in enumerate(BIG)}
        maa1 = sb("maa1", [P, NT, NMIX * DM])
        maa2 = sb("maa2", [P, 2, C])
        dec1 = sb("dec1", [P, NT, DD])
        dec2 = sb("dec2", [DD + 1, C])
        vec = sb("vec", [P, len(VECS), NT])
        V = {n: vec[:, i] for i, n in enumerate(VECS)}
        shifts = sb("shifts", [P, B, 2, NT])
        s0 = sb("s0", [P, NT, B, S])
        ob_rows = sb("ob_rows", [T, C])
        ident = sb("ident", [P, P])
        same_head = sb("same_head", [P, P])
        place = sb("place", [P, P + S - 1])
        neghalf = sb("neghalf", [P, 1])
        eps = sb("eps", [P, 1])
        x_in = sb("x_in", [T, C])
        rows = sb("rows", [T, C])
        stats = sb("stats", [T, 6])
        mv = sb("mv", [T, 2])
        small = sb("small", [T, 2])
        waiter = sb("waiter", [T, NH + 2])
        xa = sb("xa", [P, NT, T + 1])
        sx = sb("sx", [P, NT, T])
        t4 = sb("t4", [P, 2, T])
        tmp = sb("tmp", [P, 2, NT, T])
        xxx = tmp[:, 1]
        xj = sb("xj", [P, 3, NT, T])
        dt65 = sb("dt65", [DD + 1, T])
        ws = sb("ws", [P, NT, T])
        ks = sb("ks", [P, NT, T + 1])
        vt = sb("vt", [P, NT, T + 1])
        rt = sb("rt", [P, NT, T])
        gate = sb("gate", [P, NT, T])
        ruk = sb("ruk", [P, NT, T])
        y = sb("y", [T, C])
        ysq = sb("ysq", [T, C])
        hs = sb("hs", [T, 4, H])
        x2 = sb("x2", [T, C])
        lat = sb("lat", [T, C])
        rows_y = sb("rows_y", [T, C])
        x1 = sb("x1", [T, C])
        small_y = sb("small_y", [T, 2])
        lat_ob = sb("lat_ob", [T, C])
        lt = sb("lt", [P, NT, T])
        qt = sb("qt", [P, NT, T])
        mask_i = sb("mask_i", [T, NCTX], I32)
        mask_b = sb("mask_b", [T, NKEY])
        nmax = sb("nmax", [T, NH])
        rsum = sb("rsum", [T, 2, NH])
        smb = sb("smb", [T, 3, 488])
        sm = [smb[:, i, 0:NKEY] for i in range(3)]
        pts = sb("pts", [P, 2, NKT, T])
        SCAN, CTX, KEYS = NBUF * VS * T, NT * NCTX, NT * NKEY
        region = sb("region", [P, SCAN + CTX + KEYS + NKT * C])
        scan = [region[:, i * VS * T:(i + 1) * VS * T].rearrange("p (a t) -> p a t", a=VS) for i in range(NBUF)]
        ctxt = region[:, SCAN:SCAN + CTX].rearrange("p (k n) -> p k n", k=NT)
        kt = region[:, SCAN + CTX:SCAN + CTX + KEYS].rearrange("p (k n) -> p k n", k=NT)
        vv = region[:, SCAN + CTX + KEYS:].rearrange("p (k n) -> p k n", k=NKT)
        flat = wbig[:, :, :, :].rearrange("p a k n -> p (a k n)")
        w1 = flat[:, 0:NT * FF].rearrange("p (k n) -> p k n", k=NT)
        w2 = flat[:, NT * FF:2 * NT * FF].rearrange("p (k n) -> p k n", k=NF)
        at = 2 * NT * FF
        h1 = flat[:, at:at + B * NT * T].rearrange("p (b k t) -> p b k t", b=B, k=NT)
        at += 2 * NT * C
        lat_all = flat[0:T, at:at + BC * C].rearrange("p (b n) -> p b n", b=BC)
        b1v = sx[:, 0, 0:NF]
        b2_rows = ob_rows
        hid_all = region[:, 0:NF * BC * T].rearrange("p (f t) -> p f t", f=NF)

        bank = [ctx.enter_context(nc.psum_tensor(f"bank{i}", [P, 512], F32)) for i in range(8)]

        def hidden(f):
            return hid_all[:, f, :]

        def tiles(i):
            return bank[i][:, 0:NT * T].rearrange("p (k t) -> p k t", k=NT)

        names = """const_loaded weights_loaded kvw_loaded wlate_loaded xin_loaded xn_ready xnT_ready xa_ready
            sx_ready xxx_ready tp_ready t_ready m_ready mix_ready xj_ready pv_ready pk_ready pr_ready pg_ready
            vt_ready ks_ready rt_ready th_ready gate_ready v_stored vb_loaded0 vb_loaded1 vb_loaded2 vb_loaded3
            a_ready s0_put s_ready prod_ready yacc_ready d1_ready dt_ready d2_ready w_exp ws_ready
            ruk_ready rkp_ready y1_ready yT_ready y_ready gsum gmean gcen gsq gvar gsd grstd yn_ready ynT_ready
            ya_ready yg_ready wo_ready x2_ready st2 mv2 ve2 rstd2 x2n_ready xcT_ready xc_ready sxc_ready xk_ready
            kkp_ready rrp_ready kk_relu kk_ready ffn_ready rrt_ready ffg lat_ready latT_ready lt_ready latob_ready
            qp_ready qt_ready kl_ready ktl_ready vl_ready vvl_ready ctx_loaded ctx_ready ctx_kept
            mask_loaded mask_eq s_done masked probs pt_ready pt_kept pvh normed rinv ao_ready op_ready
            x1_ready ve3 rstd3 x1n_ready h1T_ready h1_ready h1_stored lat_stored st1 mv1 ve1 rstd1 init_pool
            init_dve mlp_loaded h1_back w2_loaded lat_back0 lat_back1 lat_back2 lat_back3 latb2_ready hp_ready
            hid_ready mo_ready y2_ready out_stored0 out_stored1 out_stored2 out_stored3""".split()
        s = {n: sem(n) for n in names}

        block = ctx.enter_context(nc.Block())

        @block.sync
        def _(sp):
            sp.dma_start(x_in[:, :], a["x"][0]).then_inc(s["xin_loaded"], 16)
            for dst, src in ((vec, "vec"), (shifts, "shifts"), (maa1, "maa1"), (dec1, "dec1"), (dec2, "dec2"),
                             (s0, "s0")):
                sp.dma_start(dst[:], a[src]).then_inc(s["const_loaded"], 16)
            sp.dma_start(maa2[:, 0, :], a["maa2"][0:P, :]).then_inc(s["const_loaded"], 16)
            sp.dma_start(maa2[0:DM, 1, :], a["maa2"][P:P + DM, :]).then_inc(s["const_loaded"], 16)
            sp.dma_start(wbig[:, 0:4], a["wbig"][:, 0:4]).then_inc(s["weights_loaded"], 16)
            sp.dma_start(ctxt, a["ctxt"][0]).then_inc(s["ctx_loaded"], 16)
            sp.dma_start(wbig[:, 8:10], a["wbig"][:, 8:10]).then_inc(s["kvw_loaded"], 16)
            sp.dma_start(mask_i[:, :], a["mask"][0:1, :].broadcast_to([T, NCTX])).then_inc(s["mask_loaded"], 16)
            sp.sem_inc(s["h1_stored"], 16)

            def rwkv(b, first=False):
                sp.wait_ge(s["vt_ready"], b + 1)
                sp.dma_start(v_scratch[bass.ds(b, 1)].rearrange("b (k p) t -> p (b k) t", p=P),
                             vt[:, :, 0:T]).then_inc(s["v_stored"], 16)
                if first:
                    sp.dma_start(wbig[:, 4:8], a["wbig"][:, 4:8]).then_inc(s["wlate_loaded"], 16)
                    sp.dma_start(wbig[:, 10:12], a["wbig"][:, 10:12]).then_inc(s["wlate_loaded"], 16)
                    sp.dma_start(ob_rows[:, :], a["out_b"].broadcast_to([T, C])).then_inc(s["wlate_loaded"], 16)
                sp.wait_ge(s["v_stored"], b * 16 + 16)
                for i in range(NCH):
                    if i >= NBUF or not first:
                        sp.wait_ge(s["yacc_ready"], b * NCH + i - NBUF + 1)
                    c, half = i // 2, i % 2
                    src = v_scratch[bass.ds(b, 1), c * P:(c + 1) * P, :].rearrange("b (h a) t -> (b h) a t", a=S)
                    src = src[:, half * VS:(half + 1) * VS, :].rearrange("h a t -> h (a t)")
                    sp.dma_start(scan[i % NBUF].rearrange("p a t -> p (a t)"),
                                 src.unsqueeze(1).broadcast_to([HT, S, VS * T])
                                 ).then_inc(s[f"vb_loaded{i % NBUF}"], 16)

            def next_loads(b, nxt):
                sp.wait_ge(s["x2_ready"], b + 1)
                sp.dma_start(x_in[:, :], a["x"][bass.ds(nxt, 1)].rearrange("b t c -> (b t) c")
                             ).then_inc(s["xin_loaded"], 16)
                sp.wait_ge(s["ctx_ready"], (b + 1) * 7)
                sp.dma_start(ctxt, a["ctxt"][bass.ds(nxt, 1)].rearrange("b p k n -> (b p) k n")
                             ).then_inc(s["ctx_loaded"], 16)

            def store_latents(b):
                sp.wait_ge(s["lat_ready"], b + 1)
                sp.dma_start(lat_scratch[bass.ds(b, 1)].rearrange("b t c -> (b t) c"), lat[:, :]
                             ).then_inc(s["lat_stored"], 16)

            def store_h1(c):
                sp.wait_ge(s["h1_ready"], c + 1)
                sp.dma_start(h1_scratch[:, bass.ds(c, 1)].rearrange("p b k t -> p (b k) t"), qt[:, :, :]
                             ).then_inc(s["h1_stored"], 16)

            rwkv(0, first=True)
            next_loads(0, 1)
            store_latents(0)
            with sp.Fori(1, B) as b:
                sp.wait_ge(s["mask_eq"], b)
                sp.dma_start(mask_i[:, :], a["mask"][bass.ds(b, 1), :].broadcast_to([T, NCTX])
                             ).then_inc(s["mask_loaded"], 16)
                rwkv(b)
                store_h1(sp.snap(b - 1))
                next_loads(b, sp.snap((b + 1) % B))
                store_latents(b)
            sp.wait_ge(s["ffn_ready"], B)
            sp.dma_start(w1, a["w1"]).then_inc(s["mlp_loaded"], 16)
            sp.wait_ge(s["lat_ready"], B)
            sp.dma_start(b1v, a["b1"]).then_inc(s["mlp_loaded"], 16)
            sp.dma_start(w2, a["w2"]).then_inc(s["w2_loaded"], 16)
            sp.wait_ge(s["vl_ready"], B)
            sp.wait_ge(s["h1_stored"], 16 * B)
            sp.dma_start(h1[:, 0:B - 1], h1_scratch[:, 0:B - 1]).then_inc(s["mlp_loaded"], 16)
            sp.wait_ge(s["latob_ready"], B)
            sp.wait_ge(s["lat_stored"], 16 * B)
            sp.dma_start(b2_rows[:, :], a["b2"].broadcast_to([T, C])).then_inc(s["w2_loaded"], 16)
            for b in range(BC):
                sp.dma_start(lat_all[:, b, :], lat_scratch[b]).then_inc(s[f"lat_back{b}"], 16)
            store_h1(B - 1)
            sp.wait_ge(s["h1_stored"], 16 * B + 16)
            sp.dma_start(h1[:, B - 1:B], h1_scratch[:, B - 1:B]).then_inc(s["h1_back"], 16)
            for b in range(BC, B):
                sp.wait_ge(s[f"out_stored{b % BC}"], 16)
                sp.dma_start(lat_all[:, b % BC, :], lat_scratch[b]).then_inc(s[f"lat_back{b % BC}"], 16)
            for b in range(BC):
                sp.wait_ge(s[f"out_stored{b}"], 16 * B // BC)

        @block.gpsimd
        def _(pool):
            g = nc.gpsimd
            g.memset(ident[:, :], 0.0).then_inc(s["init_pool"], 1)
            g.memset(same_head[:, :], 1.0).then_inc(s["init_pool"], 1)
            g.memset(place[:, :], 0.0).then_inc(s["init_pool"], 1)
            g.memset(neghalf[:, :], -0.5).then_inc(s["init_pool"], 1)
            g.memset(eps[:, :], EPS_LN).then_inc(s["init_pool"], 1)
            g.memset(ws[:, :, 0:1], 0.0).then_inc(s["init_pool"], 1)
            g.memset(ks[:, :, 0:1], 0.0).then_inc(s["init_pool"], 1)
            g.memset(vt[:, :, 0:1], 0.0).then_inc(s["init_pool"], 1)
            pool.wait_ge(s["init_pool"], 8)
            g.affine_select(out=ident[:, :], in_=ident[:, :], compare_op=ALU.not_equal, fill=1.0, base=0,
                            pattern=[[-1, P]], channel_multiplier=1).then_inc(s["init_pool"], 1)
            blocks = same_head[:, :].rearrange("p (h r) -> p h r", r=S)
            g.affine_select(out=blocks, in_=blocks, compare_op=ALU.is_ge, fill=0.0, base=0,
                            pattern=[[-S, HT], [0, S]], channel_multiplier=1).then_inc(s["init_pool"], 1)
            pool.wait_ge(s["init_pool"], 10)
            g.affine_select(out=blocks, in_=blocks, compare_op=ALU.is_ge, fill=0.0, base=S - 1,
                            pattern=[[S, HT], [0, S]], channel_multiplier=-1).then_inc(s["init_pool"], 1)
            pool.wait_ge(s["init_pool"], 11)
            g.tensor_copy(place[:, S - 1:P + S - 1].rearrange("p (h r) -> p h r", r=S)[:, :, 0:1], blocks[:, :, 0:1]
                          ).then_inc(s["init_pool"], 1)
            pool.wait_ge(s["init_pool"], 12)

            def rstd(buf, due, done, b):
                pool.wait_ge(s[due], b + 1)
                g.tensor_tensor(buf[:, 1:2], buf[:, 0:1], neghalf[0:T, :], ALU.pow).then_inc(s[done], 1)

            def latents_and_bias(c):
                pool.wait_ge(s["lat_ready"], c + 1)
                pool.wait_ge(s["wlate_loaded"], 48)
                g.tensor_tensor(lat_ob[:, :], lat[:, :], ob_rows[:, :], ALU.add).then_inc(s["latob_ready"], 1)

            def turn(b, c=None):
                rstd(small, "ve1", "rstd1", b)
                for j in range(NMIX):
                    pool.wait_ge(s["mix_ready"], b * NMIX + j + 1)
                    if j >= 3:
                        pool.wait_ge(s[("pv_ready", "pk_ready")[j - 3]], b + 1)
                    g.tensor_tensor(xj[:, j % 3], tmp[:, j % 2], xa[:, :, 1:T + 1], ALU.add).then_inc(s["xj_ready"], 1)
                if c is not None:
                    latents_and_bias(c)
                for i in range(NCH):
                    k, half, buf = i // 2, i % 2, scan[i % NBUF]
                    pool.wait_ge(s[f"vb_loaded{i % NBUF}"], b * 32 + 16 * (i // NBUF) + 16)
                    pool.wait_ge(s["ks_ready"], b + 1)
                    g.tensor_tensor(buf, buf, ks[:, k:k + 1, 0:T].broadcast_to([P, VS, T]), ALU.mult
                                    ).then_inc(s["a_ready"], 1)
                    pool.wait_ge(s["a_ready"], b * NCH + i + 1)
                    g.tensor_tensor(buf[:, :, 0:1], buf[:, :, 0:1],
                                    s0[:, k, bass.ds(b, 1), half * VS:(half + 1) * VS].rearrange("p b a -> p a b"),
                                    ALU.add).then_inc(s["s0_put"], 1)
                if c is not None:
                    rstd(small_y, "ve3", "rstd3", c)
                rstd(small, "ve2", "rstd2", b)

            turn(0)
            with pool.Fori(1, B) as b:
                turn(b, pool.snap(b - 1))
            latents_and_bias(B - 1)
            rstd(small_y, "ve3", "rstd3", B - 1)
            pool.wait_ge(s["w2_loaded"], 32)
            for b in range(B):
                pool.wait_ge(s[f"lat_back{b % BC}"], 16 * (b // BC + 1))
                g.tensor_tensor(lat_all[:, b % BC, :], lat_all[:, b % BC, :], b2_rows[:, :], ALU.add
                                ).then_inc(s["latb2_ready"], 1)

        @block.vector
        def _(dve):
            v = nc.vector
            v.memset(bank[2][:, :], 0.0).then_inc(s["init_dve"], 1)
            v.memset(bank[3][:, :], 0.0).then_inc(s["init_dve"], 1)
            v.memset(dt65[DD:DD + 1, :], 1.0).then_inc(s["init_dve"], 1)
            v.memset(mask_b[:, NCTX:NKEY], 0.0).then_inc(s["init_dve"], 1)
            dve.wait_ge(s["init_dve"], 4)
            dve.wait_ge(s["const_loaded"], 16 * 8)
            dve.wait_ge(s["init_pool"], 12)

            def layer_norm(src, n, w, done, b):
                v.bn_stats(stats[:, :], src[:, :]).then_inc(s[f"st{n}"], 1)
                dve.wait_ge(s[f"st{n}"], b + 1)
                v.memset(waiter[:, w:w + 1], 0.0)
                v.bn_aggr(mv[:, :], stats[:, :]).then_inc(s[f"mv{n}"], 1)
                dve.wait_ge(s[f"mv{n}"], b + 1)
                v.tensor_scalar(small[:, 0:1], mv[:, 1:2], EPS_LN, None, ALU.add).then_inc(s[f"ve{n}"], 1)
                dve.wait_ge(s[f"rstd{n}"], b + 1)
                v.tensor_scalar(rows[:, :], src[:, :], mv[:, 0:1], small[:, 1:2], ALU.subtract, ALU.mult
                                ).then_inc(s[done], 1)

            def shift(b):
                dve.wait_ge(s["xa_ready"], b + 1)
                v.tensor_tensor(sx[:, :, :], xa[:, :, 0:T], xa[:, :, 1:T + 1], ALU.subtract).then_inc(s["sx_ready"], 1)
                dve.wait_ge(s["sx_ready"], b + 1)
                for k in range(NT):
                    i = v.scalar_tensor_tensor(out=xxx[:, k, :], in0=sx[:, k, :], scalar=V["maa_x"][:, k:k + 1],
                                               in1=xa[:, k, 1:T + 1], op0=ALU.mult, op1=ALU.add)
                i.then_inc(s["xxx_ready"], 1)

            def mix(b, j):
                dve.wait_ge(s["m_ready"], b * NMIX + j + 1)
                if j >= 2:
                    dve.wait_ge(s["xj_ready"], b * NMIX + j - 1)
                for k in range(NT):
                    i = v.scalar_tensor_tensor(out=tmp[:, j % 2, k, :], in0=tiles(MIX_BANK[j])[:, k, :],
                                               scalar=V["maa_" + "vkwrg"[j]][:, k:k + 1], in1=sx[:, k, :],
                                               op0=ALU.add, op1=ALU.mult)
                i.then_inc(s["mix_ready"], 1)

            def own_token(b):
                dve.wait_ge(s["rt_ready"], b + 1)
                dve.wait_ge(s["ks_ready"], b + 1)
                for k in range(NT):
                    i = v.scalar_tensor_tensor(out=ruk[:, k, :], in0=ks[:, k, 1:T + 1],
                                               scalar=V["faaaa"][:, k:k + 1], in1=rt[:, k, :],
                                               op0=ALU.mult, op1=ALU.mult)
                i.then_inc(s["ruk_ready"], 1)

            def gating(b):
                dve.wait_ge(s["th_ready"], b + 1)
                v.scalar_tensor_tensor(out=gate[:, :, :], in0=gate[:, :, :], scalar=1.0, in1=tiles(7),
                                       op0=ALU.add, op1=ALU.mult).then_inc(s["gate_ready"], 1)

            def own_values(b):
                dve.wait_ge(s["rkp_ready"], b + 1)
                v.tensor_tensor(ruk[:, :, :], tiles(5), vt[:, :, 1:T + 1], ALU.mult).then_inc(s["y1_ready"], 1)

            def scan_chunk(b, i, between=lambda: None):
                c, buf = i // 2, scan[i % NBUF]
                dve.wait_ge(s["s0_put"], b * NCH + i + 1)
                dve.wait_ge(s["ws_ready"], b + 1)
                for q in range(VS):
                    n = v.tensor_tensor_scan(buf[:, q, :], ws[:, c, :], buf[:, q, :], 0.0, ALU.mult, ALU.add)
                n.then_inc(s["s_ready"], 1)
                between()
                dve.wait_ge(s["s_ready"], b * NCH + i + 1)
                v.tensor_tensor(buf, buf, rt[:, c:c + 1, :].broadcast_to([P, VS, T]), ALU.mult
                                ).then_inc(s["prod_ready"], 1)

            def group_norm(b):
                yh = y[:, :].rearrange("p (h a) -> p h a", a=S)
                sqh = ysq[:, :].rearrange("p (h a) -> p h a", a=S)

                def per_head(ap):
                    return ap.unsqueeze(2).broadcast_to([T, H, S])
                dve.wait_ge(s["yacc_ready"], b * NCH + NCH)
                dve.wait_ge(s["y1_ready"], b + 1)
                v.tensor_tensor(ruk[:, :, :], ruk[:, :, :], tiles(7), ALU.add).then_inc(s["yT_ready"], 1)
                dve.wait_ge(s["y_ready"], b + 1)
                y_rows = bank[6][0:T, :].rearrange("p (h a) -> p h a", a=S)
                v.tensor_reduce(hs[:, 0, :], y_rows, AX.X, ALU.add).then_inc(s["gsum"], 1)
                dve.wait_ge(s["gsum"], b + 1)
                v.tensor_scalar(hs[:, 1, :], hs[:, 0, :], 1.0 / S, None, ALU.mult).then_inc(s["gmean"], 1)
                dve.wait_ge(s["gmean"], b + 1)
                v.tensor_tensor(yh, y_rows, per_head(hs[:, 1, :]), ALU.subtract).then_inc(s["gcen"], 1)
                dve.wait_ge(s["gcen"], b + 1)
                v.tensor_tensor(sqh, yh, yh, ALU.mult).then_inc(s["gsq"], 1)
                dve.wait_ge(s["gsq"], b + 1)
                v.tensor_reduce(hs[:, 2, :], sqh, AX.X, ALU.add).then_inc(s["gvar"], 1)
                dve.wait_ge(s["gsd"], b + 1)
                v.reciprocal(hs[:, 3, :], hs[:, 0, :]).then_inc(s["grstd"], 1)
                dve.wait_ge(s["grstd"], b + 1)
                v.tensor_tensor(rows[:, :].rearrange("p (h a) -> p h a", a=S), yh, per_head(hs[:, 3, :]), ALU.mult
                                ).then_inc(s["yn_ready"], 1)

            def gated(b):
                dve.wait_ge(s["ya_ready"], b + 1)
                v.scalar_tensor_tensor(out=ruk[:, :, :], in0=ruk[:, :, :], scalar=0.5, in1=gate[:, :, :],
                                       op0=ALU.mult, op1=ALU.mult).then_inc(s["yg_ready"], 1)

            def channel_mix(b):
                dve.wait_ge(s["wo_ready"], b + 1)
                v.tensor_tensor(x2[:, :], x_in[:, :], bank[5][0:T, :], ALU.add).then_inc(s["x2_ready"], 1)
                dve.wait_ge(s["x2_ready"], b + 1)
                layer_norm(x2, 2, 1, "x2n_ready", b)
                dve.wait_ge(s["xc_ready"], b + 1)
                v.tensor_tensor(sx[:, :, :], xa[:, :, 0:T], xa[:, :, 1:T + 1], ALU.subtract
                                ).then_inc(s["sxc_ready"], 1)
                dve.wait_ge(s["sxc_ready"], b + 1)
                for m, w in enumerate(("fmaa_k", "fmaa_r")):
                    for k in range(NT):
                        i = v.scalar_tensor_tensor(out=xj[:, m, k, :], in0=sx[:, k, :], scalar=V[w][:, k:k + 1],
                                                   in1=xa[:, k, 1:T + 1], op0=ALU.mult, op1=ALU.add)
                    i.then_inc(s["xk_ready"], 1)

            def latents(b, first=False):
                dve.wait_ge(s["kk_relu"], b + 1)
                v.tensor_tensor(tmp[:, 1], tmp[:, 0], tmp[:, 0], ALU.mult).then_inc(s["kk_ready"], 1)
                dve.wait_ge(s["rrt_ready"], b + 1)
                dve.wait_ge(s["ffn_ready"], b + 1)
                v.scalar_tensor_tensor(out=y[:, :], in0=ysq[:, :], scalar=1.0, in1=bank[6][0:T, :], op0=ALU.add,
                                       op1=ALU.mult).then_inc(s["ffg"], 1)
                dve.wait_ge(s["ffg"], b + 1)
                if not first:
                    dve.wait_ge(s["lat_stored"], b * 16)
                    dve.wait_ge(s["latob_ready"], b)
                v.scalar_tensor_tensor(out=lat[:, :], in0=y[:, :], scalar=0.5, in1=x2[:, :], op0=ALU.mult,
                                       op1=ALU.add).then_inc(s["lat_ready"], 1)

            def mask(c):
                dve.wait_ge(s["mask_loaded"], 16 * c + 16)
                v.tensor_scalar(mask_b[:, 0:NCTX], mask_i[:, :], 0.0, MASKED, ALU.is_equal, ALU.mult
                                ).then_inc(s["mask_eq"], 1)

            def head(c, h):
                if h == 0:
                    dve.wait_ge(s["mask_eq"], c + 1)
                if h < NH:
                    dve.wait_ge(s["s_done"], c * NH + h + 1)
                    if h >= 3:
                        dve.wait_ge(s["pt_ready"], c * NH + h - 2)
                    v.memset(waiter[:, h + 2:h + 3], 0.0)
                    v.tensor_tensor_reduce(sm[h % 3], bank[h % 2][0:T, 0:NKEY], mask_b[:, :],
                                           -1.0 / DH, 3e38, ALU.add, ALU.min, nmax[:, h:h + 1]
                                           ).then_inc(s["masked"], 1)
                if h >= 1:
                    g = h - 1
                    dve.wait_ge(s["probs"], c * NH + g + 1)
                    v.reciprocal(rsum[:, 1, g:g + 1], rsum[:, 0, g:g + 1]).then_inc(s["rinv"], 1)
                    dve.wait_ge(s["rinv"], c * NH + g + 1)
                    v.tensor_scalar(sm[g % 3], sm[g % 3], rsum[:, 1, g:g + 1], None, ALU.mult
                                    ).then_inc(s["normed"], 1)

            def rms_norm(c):
                dve.wait_ge(s["op_ready"], c + 1)
                dve.wait_ge(s["latob_ready"], c + 1)
                v.tensor_tensor(x1[:, :], bank[1][0:T, :], lat_ob[:, :], ALU.add).then_inc(s["x1_ready"], 1)
                dve.wait_ge(s["x1_ready"], c + 1)
                v.tensor_tensor_reduce(rows_y[:, :], x1[:, :], x1[:, :], 1.0 / C, EPS_RMS, ALU.mult, ALU.add,
                                       small_y[:, 0:1]).then_inc(s["ve3"], 1)
                dve.wait_ge(s["rstd3"], c + 1)
                v.tensor_scalar(rows_y[:, :], x1[:, :], small_y[:, 1:2], None, ALU.mult).then_inc(s["x1n_ready"], 1)

            def turn(b, c=None):
                def y_head(*hs_):
                    if c is not None:
                        for h in hs_:
                            head(c, h)
                dve.wait_ge(s["xin_loaded"], 16 * b + 16)
                layer_norm(x_in, 1, 0, "xn_ready", b)
                if c is not None:
                    mask(c)
                shift(b)
                mix(b, MIX_V)
                mix(b, MIX_K)
                y_head(0)
                mix(b, MIX_W)
                y_head(1)
                mix(b, MIX_R)
                y_head(2)
                mix(b, MIX_G)
                y_head(3, 4)
                own_token(b)
                y_head(5)
                gating(b)
                y_head(6)
                own_values(b)
                y_head(7)
                for i in range(4):
                    y_head(8 + 2 * i)
                    scan_chunk(b, i, lambda: y_head(9 + 2 * i))
                y_head(16)
                scan_chunk(b, 4)
                scan_chunk(b, 5)
                scan_chunk(b, 6)
                scan_chunk(b, 7)
                group_norm(b)
                if c is not None:
                    rms_norm(c)
                gated(b)
                channel_mix(b)
                latents(b, first=c is None)

            turn(0)
            with dve.Fori(1, B) as b:
                turn(b, dve.snap(b - 1))
            mask(B - 1)
            for h in range(NH + 1):
                head(B - 1, h)
            rms_norm(B - 1)
            for b in range(B):
                dve.wait_ge(s["mo_ready"], b + 1)
                dve.wait_ge(s["latb2_ready"], b + 1)
                buf = lat_all[:, b % BC, :]
                v.tensor_tensor(buf, bank[4 + b % 2][0:T, :], buf, ALU.add).then_inc(s["y2_ready"], 1)

        @block.scalar
        def _(act):
            c_ = nc.scalar
            act.wait_ge(s["const_loaded"], 16 * 8)
            act.wait_ge(s["init_pool"], 12)

            def columns(dst, src, scale, bias, done):
                for k in range(NT):
                    kw = {"bias": V[bias][:, k:k + 1]}
                    if scale is not None:
                        kw["scale"] = V[scale][:, k:k + 1]
                    i = c_.activation(dst[:, k, :], src[:, k, :], ACT.Identity, **kw)
                i.then_inc(s[done], 1)

            def head(c, i):
                if i < NH:
                    act.wait_ge(s["masked"], c * NH + i + 1)
                    c_.activation(sm[i % 3], sm[i % 3], ACT.Exp, bias=nmax[:, i:i + 1], scale=-1.0,
                                  accum_out=rsum[:, 0, i:i + 1]).then_inc(s["probs"], 1)
                if i >= 2:
                    g = i - 2
                    act.wait_ge(s["pt_ready"], c * NH + g + 1)
                    if g >= 2:
                        act.wait_ge(s["pvh"], c * NH + g - 1)
                    c_.copy(pts[0:KT_ROWS, g % 2], tiles(2 + g % 2)[0:KT_ROWS]).then_inc(s["pt_kept"], 1)

            def query(c):
                act.wait_ge(s["h1_stored"], c * 16 + 16)
                act.wait_ge(s["qp_ready"], c + 1)
                columns(qt, tiles(0), None, "q_b", "qt_ready")

            def latent_keys(c):
                act.wait_ge(s["kl_ready"], c + 1)
                columns(kt[:, :, NCTX:NKEY], tiles(1), None, "k_b", "ktl_ready")

            def latent_values(c):
                act.wait_ge(s["vl_ready"], c + 1)
                c_.copy(vv[0:T, 3, :], bank[2][0:T, :]).then_inc(s["vvl_ready"], 1)

            def context(b, n):
                act.wait_ge(s["ctx_ready"], b * 7 + n + 1)
                src = bank[CTX_BANK[n]]
                if n < NT:
                    c_.activation(kt[:, n, 0:NCTX], src[:, 0:NCTX], ACT.Identity,
                                  bias=V["k_b"][:, n:n + 1]).then_inc(s["ctx_kept"], 1)
                else:
                    c_.copy(vv[0:KT_ROWS, n - NT, :], src[0:KT_ROWS, :]).then_inc(s["ctx_kept"], 1)

            def attention_output(c):
                act.wait_ge(s["pvh"], c * NH + NH)
                columns(lt, tiles(4), None, "v_b", "ao_ready")

            def mlp_input(c):
                act.wait_ge(s["h1T_ready"], c + 1)
                for k in range(NT):
                    i = c_.activation(qt[:, k, :], tiles(0)[:, k, :], ACT.Copy, scale=V["post_w"][:, k:k + 1])
                i.then_inc(s["h1_ready"], 1)

            def turn(b, c=None):
                def y_head(*hs_):
                    if c is not None:
                        for h in hs_:
                            head(c, h)
                c_.copy(xa[:, :, 0:1], shifts[:, bass.ds(b, 1), 1, :].rearrange("p b k -> p k b"))
                if c is not None:
                    query(c)
                act.wait_ge(s["xnT_ready"], b + 1)
                columns(xa[:, :, 1:T + 1], tiles(5), "ln1_w", "ln1_b", "xa_ready")
                if c is not None:
                    latent_keys(c)
                act.wait_ge(s["tp_ready"], b + 1)
                c_.activation(t4[:, 0, :], bank[6][:, 0:T], ACT.Tanh)
                c_.activation(t4[0:DM, 1, :], bank[6][0:DM, T:2 * T], ACT.Tanh).then_inc(s["t_ready"], 1)
                if c is not None:
                    latent_values(c)
                y_head(0)
                act.wait_ge(s["pv_ready"], b + 1)
                c_.copy(vt[:, :, 1:T + 1], tiles(7)).then_inc(s["vt_ready"], 1)
                y_head(1)
                act.wait_ge(s["pk_ready"], b + 1)
                c_.copy(ks[:, :, 1:T + 1], tiles(6)).then_inc(s["ks_ready"], 1)
                y_head(2)
                act.wait_ge(s["d1_ready"], b + 1)
                c_.activation(dt65[0:DD, :], bank[5][0:DD, 0:T], ACT.Tanh).then_inc(s["dt_ready"], 1)
                y_head(3)
                act.wait_ge(s["pr_ready"], b + 1)
                c_.copy(rt[:, :, :], tiles(7)).then_inc(s["rt_ready"], 1)
                act.wait_ge(s["d2_ready"], b + 1)
                c_.activation(gate[:, :, :], tiles(5), ACT.Exp).then_inc(s["w_exp"], 1)
                act.wait_ge(s["w_exp"], b + 1)
                c_.activation(ws[:, :, 1:T], gate[:, :, 0:T - 1], ACT.Exp, scale=-1.0).then_inc(s["ws_ready"], 1)
                y_head(4)
                act.wait_ge(s["pg_ready"], b + 1)
                act.wait_ge(s["ws_ready"], b + 1)
                c_.activation(gate[:, :, :], tiles(7), ACT.Tanh, scale=0.5).then_inc(s["th_ready"], 1)
                y_head(*range(5, NH + 2))
                if c is not None:
                    attention_output(c)
                context(b, 0)
                context(b, 1)
                context(b, 2)
                context(b, 3)
                act.wait_ge(s["gvar"], b + 1)
                c_.activation(hs[:, 0, :], hs[:, 2, :], ACT.Sqrt, bias=eps[0:T, :], scale=1.0 / S
                              ).then_inc(s["gsd"], 1)
                act.wait_ge(s["ynT_ready"], b + 1)
                columns(ruk, tiles(6), "gn_w", "gn_b", "ya_ready")
                context(b, 4)
                if c is not None:
                    mlp_input(c)
                context(b, 5)
                c_.copy(xa[:, :, 0:1], shifts[:, bass.ds(b, 1), 0, :].rearrange("p b k -> p k b"))
                act.wait_ge(s["xcT_ready"], b + 1)
                columns(xa[:, :, 1:T + 1], tiles(6), "ln2_w", "ln2_b", "xc_ready")
                context(b, 6)
                act.wait_ge(s["kkp_ready"], b + 1)
                c_.activation(tmp[:, 0], tiles(7), ACT.Relu).then_inc(s["kk_relu"], 1)
                act.wait_ge(s["rrp_ready"], b + 1)
                c_.activation(ysq[:, :], bank[5][0:T, :], ACT.Tanh, scale=0.5).then_inc(s["rrt_ready"], 1)
                act.wait_ge(s["latT_ready"], b + 1)
                c_.copy(lt[:, :, :], tiles(4)).then_inc(s["lt_ready"], 1)

            turn(0)
            with act.Fori(1, B) as b:
                turn(b, act.snap(b - 1))
            query(B - 1)
            latent_keys(B - 1)
            latent_values(B - 1)
            for i in range(NH + 2):
                head(B - 1, i)
            attention_output(B - 1)
            mlp_input(B - 1)
            act.wait_ge(s["mlp_loaded"], 48)
            act.wait_ge(s["ctx_loaded"], 16 * (B + 1))
            for n in range(2):
                for f in range(NF):
                    act.wait_ge(s["hp_ready"], n * NF + f + 1)
                    if n:
                        act.wait_ge(s["mo_ready"], BC)
                    c_.activation(hidden(f), bank[f % 4][:, 0:BC * T], ACT.Gelu_apprx_tanh,
                                  bias=b1v[:, f:f + 1]).then_inc(s["hid_ready"], 1)
            for b in range(B):
                act.wait_ge(s["y2_ready"], b + 1)
                act.dma_start(out[b], lat_all[:, b % BC, :]).then_inc(s[f"out_stored{b % BC}"], 16)

        @block.tensor
        def _(pe):
            t_ = nc.tensor

            def turned(dst, src, done):
                for k in range(NT):
                    i = t_.transpose(tiles(dst)[:, k, :], src[:, k * P:(k + 1) * P], ident[0:T, 0:T])
                i.then_inc(s[done], 1)

            def to_columns(dst, w, x, done):
                for m in range(NT):
                    for k in range(NT):
                        i = t_.matmul(tiles(dst)[:, m, :], w[:, k, m * P:(m + 1) * P], x[:, k, :],
                                      start=k == 0, stop=k == NT - 1)
                i.then_inc(s[done], 1)

            def to_rows(dst, w, x, done, m=T):
                for k in range(NT):
                    i = t_.matmul(bank[dst][0:m, :], x[:, k, :], w[:, k, :], start=k == 0, stop=k == NT - 1)
                i.then_inc(s[done], 1)

            def adapter_inputs(b):
                pe.wait_ge(s["xxx_ready"], b + 1)
                for k in range(NT):
                    t_.matmul(bank[6][:, 0:T], maa1[:, k, 0:P], xxx[:, k, :], start=k == 0, stop=k == NT - 1)
                for k in range(NT):
                    i = t_.matmul(bank[6][0:DM, T:2 * T], maa1[:, k, P:P + DM], xxx[:, k, :],
                                  start=k == 0, stop=k == NT - 1)
                i.then_inc(s["tp_ready"], 1)

            def adapter(j):
                r = j % 4 * DM
                for m in range(NT):
                    i = t_.matmul(tiles(MIX_BANK[j])[:, m, :], maa2[r:r + DM, j // 4, m * P:(m + 1) * P],
                                  t4[r:r + DM, j // 4, :], start=True, stop=True)
                i.then_inc(s["m_ready"], 1)

            def context(b, n):
                if n == 0:
                    pe.wait_ge(s["ctx_loaded"], 16 * b + 16)
                if n >= 2:
                    pe.wait_ge(s["ctx_kept"], b * 7 + n - 1)
                dst = bank[CTX_BANK[n]]
                for k in range(NT):
                    if n < NT:
                        i = t_.matmul(dst[:, 0:NCTX], W["kw"][:, k, n * P:(n + 1) * P], ctxt[:, k, :],
                                      start=k == 0, stop=k == NT - 1)
                    else:
                        r = (n - NT) * KT_ROWS
                        i = t_.matmul(dst[0:KT_ROWS, :], ctxt[:, k, r:r + KT_ROWS], W["vw"][:, k, :],
                                      start=k == 0, stop=k == NT - 1)
                i.then_inc(s["ctx_ready"], 1)

            def sum_chunk(b, i):
                pe.wait_ge(s["prod_ready"], b * NCH + i + 1)
                for q in range(VS):
                    a = i % 2 * VS + q
                    n = t_.matmul(tiles(7)[:, i // 2, :], place[:, S - 1 - a:S - 1 - a + P], scan[i % NBUF][:, q, :],
                                  start=a == 0, stop=a == S - 1)
                n.then_inc(s["yacc_ready"], 1)

            def head(c, i):
                if i < NH:
                    g, r = i // HG, i % HG * DH
                    if i >= 2:
                        pe.wait_ge(s["masked"], c * NH + i - 1)
                    t_.matmul(bank[i % 2][0:T, 0:NKEY], qt[r:r + DH, g, :], kt[r:r + DH, g, :],
                              start=True, stop=True).then_inc(s["s_done"], 1)
                if 2 <= i < NH + 2:
                    g = i - 2
                    pe.wait_ge(s["normed"], c * NH + g + 1)
                    if g >= 2:
                        pe.wait_ge(s["pt_kept"], c * NH + g - 1)
                    for j in range(NKT):
                        n = KT_ROWS if j < 3 else T
                        m = t_.transpose(tiles(2 + g % 2)[0:n, j, :], sm[g % 3][:, j * KT_ROWS:j * KT_ROWS + n],
                                         ident[0:T, 0:T])
                    m.then_inc(s["pt_ready"], 1)
                if i >= 3:
                    g = i - 3
                    pe.wait_ge(s["pt_kept"], c * NH + g + 1)
                    for j in range(NKT):
                        n = KT_ROWS if j < 3 else T
                        r = g % HG * DH
                        m = t_.matmul(tiles(4)[r:r + DH, g // HG, :], vv[0:n, j, g * DH:(g + 1) * DH],
                                      pts[0:n, g % 2, j, :], start=j == 0, stop=j == NKT - 1)
                    m.then_inc(s["pvh"], 1)

            def query(c):
                pe.wait_ge(s["lt_ready"], c + 1)
                to_columns(0, W["qw"], lt, "qp_ready")

            def before_heads(c):
                pe.wait_ge(s["qt_ready"], c + 1)
                pe.wait_ge(s["ktl_ready"], c + 1)
                pe.wait_ge(s["vvl_ready"], c + 1)
                pe.wait_ge(s["ctx_kept"], c * 7 + 7)

            def output_projection(c):
                pe.wait_ge(s["ao_ready"], c + 1)
                to_rows(1, W["ow"], lt, "op_ready")

            def mlp_input(c):
                pe.wait_ge(s["x1n_ready"], c + 1)
                turned(0, rows_y, "h1T_ready")

            def turn(b, c=None):
                def y_head(*hs_):
                    if c is not None:
                        for h in hs_:
                            head(c, h)
                if c is not None:
                    query(c)
                pe.wait_ge(s["xn_ready"], b + 1)
                turned(5, rows, "xnT_ready")
                if c is not None:
                    to_columns(1, W["kw"], lt, "kl_ready")
                adapter_inputs(b)
                if c is not None:
                    to_rows(2, W["vw"], lt, "vl_ready")
                pe.wait_ge(s["t_ready"], b + 1)
                adapter(MIX_V)
                adapter(MIX_K)
                if c is not None:
                    before_heads(c)
                y_head(0)
                adapter(MIX_W)
                if c is None:
                    pe.wait_ge(s["weights_loaded"], 16)
                pe.wait_ge(s["xj_ready"], b * NMIX + MIX_V + 1)
                to_columns(7, W["Wv"], xj[:, MIX_V % 3], "pv_ready")
                y_head(1)
                pe.wait_ge(s["mix_ready"], b * NMIX + MIX_K + 1)
                adapter(MIX_R)
                pe.wait_ge(s["mix_ready"], b * NMIX + MIX_W + 1)
                pe.wait_ge(s["xj_ready"], b * NMIX + MIX_K + 1)
                to_columns(6, W["Wk"], xj[:, MIX_K % 3], "pk_ready")
                y_head(2)
                pe.wait_ge(s["vt_ready"], b + 1)
                adapter(MIX_G)
                pe.wait_ge(s["mix_ready"], b * NMIX + MIX_R + 1)
                pe.wait_ge(s["xj_ready"], b * NMIX + MIX_W + 1)
                for k in range(NT):
                    i = t_.matmul(bank[5][0:DD, 0:T], dec1[:, k, :], xj[:, MIX_W % 3, k, :],
                                  start=k == 0, stop=k == NT - 1)
                i.then_inc(s["d1_ready"], 1)
                y_head(3)
                pe.wait_ge(s["mix_ready"], b * NMIX + MIX_G + 1)
                pe.wait_ge(s["xj_ready"], b * NMIX + MIX_R + 1)
                to_columns(7, W["Wr"], xj[:, MIX_R % 3], "pr_ready")
                pe.wait_ge(s["dt_ready"], b + 1)
                for m in range(NT):
                    i = t_.matmul(tiles(5)[:, m, :], dec2[:, m * P:(m + 1) * P], dt65[:, :], start=True, stop=True)
                i.then_inc(s["d2_ready"], 1)
                y_head(4)
                pe.wait_ge(s["rt_ready"], b + 1)
                pe.wait_ge(s["xj_ready"], b * NMIX + MIX_G + 1)
                to_columns(7, W["Wg"], xj[:, MIX_G % 3], "pg_ready")
                y_head(5)
                y_head(6)
                pe.wait_ge(s["ruk_ready"], b + 1)
                pe.wait_ge(s["w_exp"], b + 1)
                for k in range(NT):
                    i = t_.matmul(tiles(5)[:, k, :], same_head[:, :], ruk[:, k, :], start=True, stop=True)
                i.then_inc(s["rkp_ready"], 1)
                y_head(7, 8, 9)
                pe.wait_ge(s["gate_ready"], b + 1)
                if c is None:
                    pe.wait_ge(s["kvw_loaded"], 16)
                for i in range(NCH):
                    sum_chunk(b, i)
                    if i < 4:
                        y_head(10 + 2 * i, 11 + 2 * i)
                    if i == 4:
                        y_head(18)
                        context(b, 0)
                    if i == 6:
                        context(b, 1)
                if c is not None:
                    output_projection(c)
                context(b, 2)
                pe.wait_ge(s["yT_ready"], b + 1)
                pe.wait_ge(s["ks_ready"], b + 1)
                for k in range(NT):
                    i = t_.transpose(bank[6][0:T, k * P:(k + 1) * P], ruk[:, k, :], ident[:, :])
                i.then_inc(s["y_ready"], 1)
                context(b, 3)
                pe.wait_ge(s["yn_ready"], b + 1)
                turned(6, rows, "ynT_ready")
                context(b, 4)
                pe.wait_ge(s["yg_ready"], b + 1)
                if c is None:
                    pe.wait_ge(s["wlate_loaded"], 48)
                to_rows(5, W["Wo"], ruk, "wo_ready")
                if c is not None:
                    mlp_input(c)
                context(b, 5)
                pe.wait_ge(s["x2n_ready"], b + 1)
                turned(6, rows, "xcT_ready")
                context(b, 6)
                pe.wait_ge(s["xk_ready"], 2 * b + 1)
                to_columns(7, W["fWk"], xj[:, 0], "kkp_ready")
                pe.wait_ge(s["xk_ready"], 2 * b + 2)
                to_rows(5, W["fWr"], xj[:, 1], "rrp_ready")
                pe.wait_ge(s["kk_ready"], b + 1)
                to_rows(6, W["fWv"], tmp[:, 1], "ffn_ready")
                pe.wait_ge(s["lat_ready"], b + 1)
                turned(4, lat, "latT_ready")

            pe.wait_ge(s["init_pool"], 12)
            pe.wait_ge(s["init_dve"], 4)
            pe.wait_ge(s["const_loaded"], 16 * 8)
            turn(0)
            with pe.Fori(1, B) as b:
                turn(b, pe.snap(b - 1))
            query(B - 1)
            to_columns(1, W["kw"], lt, "kl_ready")
            to_rows(2, W["vw"], lt, "vl_ready")
            before_heads(B - 1)
            for i in range(NH + 3):
                head(B - 1, i)
            output_projection(B - 1)
            mlp_input(B - 1)
            pe.wait_ge(s["mlp_loaded"], 48)
            pe.wait_ge(s["h1_ready"], B)
            for n in range(2):
                if n:
                    pe.wait_ge(s["h1_back"], 16)
                for f in range(NF):
                    if n * NF + f >= 4:
                        pe.wait_ge(s["hid_ready"], n * NF + f - 3)
                    for k in range(NT):
                        i = t_.matmul(bank[f % 4][:, 0:BC * T], w1[:, k, f * P:(f + 1) * P],
                                      h1[:, n * BC:(n + 1) * BC, k, :], start=k == 0, stop=k == NT - 1)
                    i.then_inc(s["hp_ready"], 1)
                pe.wait_ge(s["w2_loaded"], 32)
                for b in range(BC):
                    m = n * BC + b
                    if m >= 2:
                        pe.wait_ge(s["y2_ready"], m - 1)
                    for f in range(NF):
                        if b == 0:
                            pe.wait_ge(s["hid_ready"], n * NF + f + 1)
                        i = t_.matmul(bank[4 + m % 2][0:T, :], hidden(f)[:, b * T:(b + 1) * T], w2[:, f, :],
                                      start=f == 0, stop=f == NF - 1)
                    i.then_inc(s["mo_ready"], 1)


def kernel(**inputs):
    import numpy as np
    import concourse.bacc as bacc
    from concourse.bass_utils import run_bass_kernel_spmd as run

    i = {k: np.asarray(v) for k, v in inputs.items()}
    L0 = {k[len("L0_xattn_"):]: v for k, v in i.items() if k.startswith("L0_xattn_")}
    L1 = {k[len("L1_xattn_"):]: v for k, v in i.items() if k.startswith("L1_xattn_")}

    def cols(v):
        return v.reshape(-1, P).T

    def wt(w):
        return w.reshape(-1, P, w.shape[1]).transpose(1, 0, 2)

    kv_w = L1["kv_w"].reshape(C, C, 2)
    kv_b = L1["kv_b"].reshape(C, 2)
    vecs = dict(ln1_w=L0["ln1_w"], ln1_b=L0["ln1_b"], ln2_w=L0["ln2_w"], ln2_b=L0["ln2_b"], maa_x=L0["maa_x"],
                faaaa=L0["faaaa"].reshape(C), gn_w=L0["gn_w"], gn_b=L0["gn_b"], fmaa_k=L0["fmaa_k"],
                fmaa_r=L0["fmaa_r"], q_b=L1["q_b"], k_b=kv_b[:, 0], v_b=kv_b[:, 1], post_w=L1["postnorm_w"],
                **{"maa_" + n: L0["maa_" + n] for n in "vkwrg"})
    big = dict(Wv=L0["Wv"].T, Wk=L0["Wk"].T, Wr=L0["Wr"].T, Wg=L0["Wg"].T, Wo=L0["Wo"].T, fWk=L0["fWk"].T,
               fWr=L0["fWr"].T, fWv=L0["fWv"].T, kw=kv_w[:, :, 0], vw=kv_w[:, :, 1], qw=L1["q_w"], ow=L1["out_w"])
    order = [2, 1, 0, 3, 4]
    maa1 = L0["maa_w1"].reshape(C, NMIX, DM)[:, order].reshape(C, NMIX * DM)
    c = i["ctx_2048"]
    arrays = dict(
        x=i["x"],
        vec=np.stack([cols(vecs[n]) for n in VECS], 1),
        shifts=c[:, 0:2].reshape(B, 2, NT, P).transpose(3, 0, 1, 2),
        s0=c[:, 2:2 + S].reshape(B, NT, P, S).transpose(2, 1, 0, 3),
        ctxt=c.reshape(B, NCTX, NT, P).transpose(0, 3, 2, 1),
        mask=i["mask_BxS2_ik0"],
        maa1=wt(maa1),
        maa2=L0["maa_w2"][order].reshape(NMIX * DM, C),
        dec1=wt(L0["decay_w1"]),
        dec2=np.concatenate([L0["decay_w2"], L0["time_decay"][None]], 0),
        wbig=np.stack([wt(big[n]) for n in BIG], 1),
        w1=wt(L1["mlp_w1"]), w2=wt(L1["mlp_w2"]), b1=cols(L1["mlp_b1"]),
        b2=L1["mlp_b2"][None], out_b=L1["out_b"][None],
    )
    nc = bacc.Bacc("TRN2", target_bir_lowering=False, num_devices=1)
    feed, aps = {}, {}
    for n, v in arrays.items():
        feed[f"in_{n}"] = np.ascontiguousarray(v)
        aps[n] = nc.dram_tensor(f"in_{n}", v.shape, mybir.dt.from_np(v.dtype), kind="ExternalInput").ap()
    out = nc.dram_tensor("out_0", (B, T, C), F32, kind="ExternalOutput").ap()
    build(nc, aps, out)
    r = run(nc, [feed], core_ids=[0])
    return r.results[0]["out_0"]
```

```python
from contextlib import ExitStack

import concourse.bass as bass
from concourse import mybir

F32 = mybir.dt.float32
F32R = mybir.dt.float32r
I32 = mybir.dt.int32
ALU = mybir.AluOpType
ACT = mybir.ActivationFunctionType
AX = mybir.AxisListType

P = 128
B, T, C = 8, 112, 512
NT = C // P
H, S = 32, 16
HT = P // S
NCTX = 375
NKEY = NCTX + T
KT_ROWS = 125
NKT = 4
NH, DH = 16, 32
HG = P // DH
FF = 4 * C
NF = FF // P
DM, DD, NMIX = 32, 64, 5
VS = 8
NCH = NT * S // VS
NBUF = 4
BC = 4
LATE = NCH - NBUF + 2
EPS_LN, EPS_RMS = 1e-5, 1e-6
MASKED = -1e30

MIX_V, MIX_K, MIX_W, MIX_R, MIX_G = range(NMIX)
MIX_BANK = (7, 5, 6, 5, 7)
OUT_BANK = (2, 3, 4, 7)
HID_BANK = (5, 6)
CTX_BANK = (2, 3, 2, 3, 2, 3, 2)
VECS = ["ln1_w", "ln1_b", "ln2_w", "ln2_b", "maa_x", "faaaa", "gn_w", "gn_b", "fmaa_k", "fmaa_r",
        "q_b", "k_b", "v_b", "post_w", "maa_v", "maa_k", "maa_w", "maa_r", "maa_g"]
BIG = ["Wv", "Wk", "Wr", "Wg", "Wo", "fWk", "fWr", "fWv", "kw", "vw", "qw", "ow"]


def build(nc, a, out):
    with ExitStack() as ctx:
        address = {}

        def sb(name, shape, dt=F32):
            buf = ctx.enter_context(nc.sbuf_tensor(name, shape, dt))
            size = 4
            for n in shape[1:]:
                size *= n
            address[name] = nc.sbuf_base - size
            return buf

        def over(name, base, shape, skip=0):
            return nc.alloc_sbuf_tensor_at(name, shape, F32R, offset=address[base] + 4 * skip)

        def sem(name):
            return ctx.enter_context(nc.semaphore(name))

        def dram(name, shape):
            return nc.dram_tensor(name, shape, F32, kind="Internal").ap()

        v_scratch = dram("v_scratch", (B, C, T))
        lat_scratch = dram("lat_scratch", (B, T, C))
        h1_scratch = dram("h1_scratch", (P, B - 1, NT, T))

        wbig = sb("wbig", [P, len(BIG), NT, C])
        W = {n: wbig[:, i] for i, n in enumerate(BIG)}
        maa1 = sb("maa1", [P, NT, NMIX * DM])
        maa2 = sb("maa2", [P, 2, C])
        dec1 = sb("dec1", [P, NT, DD])
        dec2 = sb("dec2", [DD + 1, C])
        vec = sb("vec", [P, len(VECS), NT])
        V = {n: vec[:, i] for i, n in enumerate(VECS)}
        shifts = sb("shifts", [P, B, 2, NT])
        s0 = sb("s0", [P, NT, B, S])
        ob_rows = sb("ob_rows", [T, C])
        ident = sb("ident", [P, P])
        same_head = sb("same_head", [P, P])
        place = sb("place", [P, HT * VS + VS - 1])
        neghalf = sb("neghalf", [P, 1])
        eps = sb("eps", [P, 1])
        table = sb("table", [1, 1])
        x_in_all = sb("x_in", [P, C])
        x_in = x_in_all[0:T, :]
        rows_all = sb("rows", [P, C])
        rows = rows_all[0:T, :]
        stats = sb("stats", [T, 6])
        mv = sb("mv", [T, 2])
        small = sb("small", [T, 2])
        waiter = sb("waiter", [T, NH + 2])
        xa = sb("xa", [P, NT, T + 1])
        sx = sb("sx", [P, NT, T])
        t4 = sb("t4", [P, 2, T])
        tmp = sb("tmp", [P, 2, NT, T])
        xxx = tmp[:, 1]
        xj = sb("xj", [P, 3, NT, T])
        dt65 = sb("dt65", [DD + 1, T])
        ws = sb("ws", [P, NT, T])
        ks = sb("ks", [P, NT, T + 1])
        vt = sb("vt", [P, NT, T + 1])
        rt = sb("rt", [P, NT, T])
        gate = sb("gate", [P, NT, T])
        ruk = sb("ruk", [P, NT, T])
        y_all = sb("y", [P, C])
        y = y_all[0:T, :]
        ysq_all = sb("ysq", [P, C])
        ysq = ysq_all[0:T, :]
        hs = sb("hs", [T, 4, H])
        x2 = y
        lat = sb("lat", [T, C])
        rows_y = sb("rows_y", [T, C])
        small_y = sb("small_y", [T, 2])
        lat_ob = sb("lat_ob", [T, C])
        x1 = lat_ob
        lt = sb("lt", [P, NT, T])
        h1_out = sb("h1_out", [P, NT, T])
        queries = sb("queries", [P, NH, T])
        mask_b = sb("mask_b", [T, NKEY])
        mask_i = mask_b[:, 0:NCTX].bitcast(I32)
        nmax = sb("nmax", [T, NH])
        rsum = sb("rsum", [T, 2, NH])
        smb = sb("smb", [T, 3, 488])
        sm = [smb[:, i, 0:NKEY] for i in range(3)]
        pts = sb("pts", [P, 2, NKT, T])
        SCAN, CTX, KEYS = NBUF * VS * T, NT * NCTX, NT * NKEY
        region = sb("region", [P, SCAN + CTX + KEYS + NKT * C])
        scan = [region[:, i * VS * T:(i + 1) * VS * T].rearrange("p (a t) -> p a t", a=VS) for i in range(NBUF)]
        ctxt = region[:, SCAN:SCAN + CTX].rearrange("p (k n) -> p k n", k=NT)
        kt = region[:, SCAN + CTX:SCAN + CTX + KEYS].rearrange("p (k n) -> p k n", k=NT)
        vv = region[:, SCAN + CTX + KEYS:].rearrange("p (k n) -> p k n", k=NKT)
        flat = wbig[:, :, :, :].rearrange("p a k n -> p (a k n)")
        w1 = flat[:, 0:NT * FF].rearrange("p (f k n) -> p f k n", f=NF, k=NT)
        w2 = flat[:, NT * FF:2 * NT * FF].rearrange("p (f n) -> p f n", f=NF)
        at = 2 * NT * FF
        h1 = flat[:, at:at + B * NT * T].rearrange("p (b k t) -> p b k t", b=B, k=NT)
        h1_hi = over("h1_hi", "region", [P, B, NT, T])
        h1_lo = over("h1_lo", "wbig", [P, B, NT, T], at)
        at += 2 * NT * C
        lat_all = flat[0:T, at:at + BC * C].rearrange("p (b n) -> p b n", b=BC)
        b1v = sx[:, 0, 0:NF]
        b2_rows = ob_rows
        w1_hi = [over("w1_hi0", "ysq", [P, NT, P]), over("w1_hi1", "xj", [P, NT, P])]
        w1_lo = [over("w1_lo0", "y", [P, NT, P]), over("w1_lo1", "xj", [P, NT, P], C)]
        w2_hi = [over("w2_hi0", "region", [P, C], SCAN), over("w2_hi1", "tmp", [P, C])]
        w2_lo = [over("w2_lo0", "x_in", [P, C]), over("w2_lo1", "rows", [P, C])]
        hid = [i[:, :, :].rearrange("p k t -> p (k t)") for i in (gate, ws)]
        hid_lo = [over("hid_lo0", "gate", [P, BC * T]), over("hid_lo1", "ws", [P, BC * T])]
        hid_hi = [over("hid_hi0", "ruk", [P, BC * T]), over("hid_hi1", "rt", [P, BC * T])]

        bank = [ctx.enter_context(nc.psum_tensor(f"bank{i}", [P, 512], F32)) for i in range(8)]

        def tiles(i):
            return bank[i][:, 0:NT * T].rearrange("p (k t) -> p k t", k=NT)

        names = """vec_loaded wv_loaded queries_zeroed const_loaded weights_loaded kvw_loaded wlate_loaded
            xin_loaded xn_ready xnT_ready xa_ready
            sx_ready xxx_ready tp_ready t_ready m_ready mix_ready xj_ready pv_ready pk_ready pr_ready pg_ready
            vt_ready ks_ready rt_ready th_ready gate_ready v_stored vb_loaded0 vb_loaded1 vb_loaded2 vb_loaded3
            a_ready s0_put s_ready prod_ready yacc_ready d1_ready dt_ready d2_ready w_exp ws_ready
            ruk_ready rkp_ready y1_ready y_ready gsum gmean gcen gsq gvar gsd grstd yn_ready ynT_ready
            ya_ready yg_ready wo_ready x2_ready st2 mv2 ve2 rstd2 x2n_ready xcT_ready xc_ready sxc_ready xk_ready
            kkp_ready rrp_ready kk_relu kk_ready ffn_ready rrt_ready ffg lat_ready latT_ready lt_ready latob_ready
            qp_ready qt_ready kl_ready ktl_ready vl_ready vvl_ready ctx_loaded ctx_ready ctx_kept
            mask_loaded mask_eq s_done masked probs pt_ready pt_kept pvh normed rinv ao_ready op_ready
            x1_ready ve3 rstd3 x1n_ready h1T_ready h1_ready h1_stored lat_stored st1 mv1 ve1 rstd1 init_pool
            init_dve mlp_loaded w2_loaded lat_back0 lat_back1 lat_back2 lat_back3 latb2_ready hp_ready
            hid_ready mo_ready h1_hi_ready h1_lo_ready w1_hi_ready w1_ready w2_hi_ready w2_ready hid_hi_ready
            hid_split step_done y2_ready out_stored0 out_stored1 out_stored2 out_stored3""".split()
        s = {n: sem(n) for n in names}

        block = ctx.enter_context(nc.Block())

        @block.sync
        def _(sp):
            sp.dma_start(x_in[:, :], a["x"][0]).then_inc(s["xin_loaded"], 16)
            sp.dma_start(vec[:], a["vec"]).then_inc(s["vec_loaded"], 16)
            sp.dma_start(shifts[:], a["shifts"]).then_inc(s["vec_loaded"], 16)
            for dst, src in ((maa1, "maa1"), (dec1, "dec1"), (dec2, "dec2"), (s0, "s0")):
                sp.dma_start(dst[:], a[src]).then_inc(s["const_loaded"], 16)
            sp.dma_start(maa2[:, 0, :], a["maa2"][0:P, :]).then_inc(s["const_loaded"], 16)
            sp.dma_start(maa2[0:DM, 1, :], a["maa2"][P:P + DM, :]).then_inc(s["const_loaded"], 16)
            sp.dma_start(wbig[:, 0:1], a["wbig"][:, 0:1]).then_inc(s["wv_loaded"], 16)
            sp.dma_start(wbig[:, 1:4], a["wbig"][:, 1:4]).then_inc(s["weights_loaded"], 16)
            sp.dma_start(ctxt, a["ctxt"][0]).then_inc(s["ctx_loaded"], 16)
            sp.dma_start(wbig[:, 8:10], a["wbig"][:, 8:10]).then_inc(s["kvw_loaded"], 16)
            sp.dma_start(mask_i[:, :], a["mask"][0:1, :].broadcast_to([T, NCTX])).then_inc(s["mask_loaded"], 16)
            sp.sem_inc(s["h1_stored"], 16)

            def rwkv(b, first=False):
                sp.wait_ge(s["vt_ready"], b + 1)
                sp.dma_start(v_scratch[bass.ds(b, 1)].rearrange("b (k p) t -> p (b k) t", p=P),
                             vt[:, :, 0:T]).then_inc(s["v_stored"], 16)
                sp.wait_ge(s["v_stored"], b * 16 + 16)
                for i in range(NCH):
                    if i >= NBUF or not first:
                        sp.wait_ge(s["yacc_ready"], b * NCH + i - NBUF + 1)
                    c, half = i // 2, i % 2
                    src = v_scratch[bass.ds(b, 1), c * P:(c + 1) * P, :].rearrange("b (h a) t -> (b h) a t", a=S)
                    src = src[:, half * VS:(half + 1) * VS, :].rearrange("h a t -> h (a t)")
                    sp.dma_start(scan[i % NBUF].rearrange("p a t -> p (a t)"),
                                 src.unsqueeze(1).broadcast_to([HT, S, VS * T])
                                 ).then_inc(s[f"vb_loaded{i % NBUF}"], 16)
                    if first and NBUF - 1 <= i < NCH - 1:
                        w = 4 + i - (NBUF - 1)
                        sp.dma_start(wbig[:, w:w + 1], a["wbig"][:, w:w + 1]).then_inc(s["wlate_loaded"], 16)
                if first:
                    sp.dma_start(wbig[:, 10:12], a["wbig"][:, 10:12]).then_inc(s["wlate_loaded"], 16)
                    sp.dma_start(ob_rows[:, :], a["out_b"].broadcast_to([T, C])).then_inc(s["wlate_loaded"], 16)

            def next_loads(b, nxt):
                sp.wait_ge(s["x2_ready"], b + 1)
                sp.dma_start(x_in[:, :], a["x"][bass.ds(nxt, 1)].rearrange("b t c -> (b t) c")
                             ).then_inc(s["xin_loaded"], 16)
                sp.wait_ge(s["ctx_ready"], (b + 1) * 7)
                sp.dma_start(ctxt, a["ctxt"][bass.ds(nxt, 1)].rearrange("b p k n -> (b p) k n")
                             ).then_inc(s["ctx_loaded"], 16)

            def store_latents(b):
                sp.wait_ge(s["lat_ready"], b + 1)
                sp.dma_start(lat_scratch[bass.ds(b, 1)].rearrange("b t c -> (b t) c"), lat[:, :]
                             ).then_inc(s["lat_stored"], 16)

            def store_h1(c):
                sp.wait_ge(s["h1_ready"], c + 1)
                sp.dma_start(h1_scratch[:, bass.ds(c, 1)].rearrange("p b k t -> p (b k) t"), h1_out[:, :, :]
                             ).then_inc(s["h1_stored"], 16)

            rwkv(0, first=True)
            next_loads(0, 1)
            store_latents(0)
            with sp.Fori(1, B) as b:
                rwkv(b)
                sp.wait_ge(s["masked"], b * NH)
                sp.dma_start(mask_i[:, :], a["mask"][bass.ds(b, 1), :].broadcast_to([T, NCTX])
                             ).then_inc(s["mask_loaded"], 16)
                store_h1(sp.snap(b - 1))
                next_loads(b, sp.snap((b + 1) % B))
                store_latents(b)
            sp.wait_ge(s["ffn_ready"], B)
            sp.dma_start(w1, a["w1"]).then_inc(s["mlp_loaded"], 16)
            sp.wait_ge(s["xxx_ready"], B + 1)
            sp.dma_start(b1v, a["b1"]).then_inc(s["mlp_loaded"], 16)
            sp.wait_ge(s["vl_ready"], B)
            sp.wait_ge(s["h1_stored"], 16 * B)
            sp.dma_start(h1[:, 0:B - 1], h1_scratch[:, 0:B - 1]).then_inc(s["mlp_loaded"], 16)
            sp.dma_start(w2, a["w2"]).then_inc(s["w2_loaded"], 16)
            sp.wait_ge(s["latob_ready"], B)
            sp.wait_ge(s["lat_stored"], 16 * B)
            sp.dma_start(b2_rows[:, :], a["b2"].broadcast_to([T, C])).then_inc(s["w2_loaded"], 16)
            for b in range(BC):
                sp.dma_start(lat_all[:, b, :], lat_scratch[b]).then_inc(s[f"lat_back{b}"], 16)
            for b in range(B):
                sp.wait_ge(s["y2_ready"], b + 1)
                sp.dma_start(out[b], lat_all[:, b % BC, :]).then_inc(s[f"out_stored{b % BC}"], 16)
                if b < BC:
                    sp.wait_ge(s[f"out_stored{b % BC}"], 16)
                    sp.dma_start(lat_all[:, b % BC, :], lat_scratch[b + BC]).then_inc(s[f"lat_back{b % BC}"], 16)
            for b in range(BC):
                sp.wait_ge(s[f"out_stored{b}"], 16 * B // BC)

        @block.gpsimd
        def _(pool):
            g = nc.gpsimd
            g.memset(ident[:, :], 0.0).then_inc(s["init_pool"], 1)
            g.memset(same_head[:, :], 1.0).then_inc(s["init_pool"], 1)
            g.memset(place[:, :], 0.0).then_inc(s["init_pool"], 1)
            g.memset(neghalf[:, :], -0.5).then_inc(s["init_pool"], 1)
            g.memset(eps[:, :], EPS_LN).then_inc(s["init_pool"], 1)
            g.memset(ws[:, :, 0:1], 0.0).then_inc(s["init_pool"], 1)
            g.memset(ks[:, :, 0:1], 0.0).then_inc(s["init_pool"], 1)
            g.memset(vt[:, :, 0:1], 0.0).then_inc(s["init_pool"], 1)
            pool.wait_ge(s["init_pool"], 8)
            g.memset(queries[:, :, :], 0.0).then_inc(s["queries_zeroed"], 1)
            g.affine_select(out=ident[:, :], in_=ident[:, :], compare_op=ALU.not_equal, fill=1.0, base=0,
                            pattern=[[-1, P]], channel_multiplier=1).then_inc(s["init_pool"], 1)
            blocks = same_head[:, :].rearrange("p (h r) -> p h r", r=S)
            g.affine_select(out=blocks, in_=blocks, compare_op=ALU.is_ge, fill=0.0, base=0,
                            pattern=[[-S, HT], [0, S]], channel_multiplier=1).then_inc(s["init_pool"], 1)
            pool.wait_ge(s["init_pool"], 10)
            g.affine_select(out=blocks, in_=blocks, compare_op=ALU.is_ge, fill=0.0, base=S - 1,
                            pattern=[[S, HT], [0, S]], channel_multiplier=-1).then_inc(s["init_pool"], 1)
            pool.wait_ge(s["init_pool"], 11)
            g.tensor_copy(place[:, VS - 1:].rearrange("p (h a) -> p h a", a=VS)[:, :, 0:1], blocks[:, :, 0:1]
                          ).then_inc(s["init_pool"], 1)
            pool.wait_ge(s["init_pool"], 12)

            def rstd(buf, due, done, b):
                pool.wait_ge(s[due], b + 1)
                g.tensor_tensor(buf[:, 1:2], buf[:, 0:1], neghalf[0:T, :], ALU.pow).then_inc(s[done], 1)

            def latents_and_bias(c):
                pool.wait_ge(s["lat_ready"], c + 1)
                pool.wait_ge(s["wlate_loaded"], 16 * LATE)
                g.tensor_tensor(lat_ob[:, :], lat[:, :], ob_rows[:, :], ALU.add).then_inc(s["latob_ready"], 1)

            def mixed(b, j):
                pool.wait_ge(s["mix_ready"], b * NMIX + j + 1)
                if j >= 3:
                    pool.wait_ge(s[("pv_ready", "pk_ready")[j - 3]], b + 1)
                g.tensor_tensor(xj[:, j % 3], tmp[:, j % 2], xa[:, :, 1:T + 1], ALU.add).then_inc(s["xj_ready"], 1)

            def scan_input(b, i):
                k, half, buf = i // 2, i % 2, scan[i % NBUF]
                pool.wait_ge(s[f"vb_loaded{i % NBUF}"], b * 32 + 16 * (i // NBUF) + 16)
                pool.wait_ge(s["ks_ready"], b + 1)
                g.tensor_tensor(buf, buf, ks[:, k:k + 1, 0:T].broadcast_to([P, VS, T]), ALU.mult
                                ).then_inc(s["a_ready"], 1)
                pool.wait_ge(s["a_ready"], b * NCH + i + 1)
                g.tensor_tensor(buf[:, :, 0:1], buf[:, :, 0:1],
                                s0[:, k, bass.ds(b, 1), half * VS:(half + 1) * VS].rearrange("p b a -> p a b"),
                                ALU.add).then_inc(s["s0_put"], 1)

            def turn(b, nxt, c=None):
                for j in range(NMIX - 1):
                    mixed(b, j)
                scan_input(b, 0)
                mixed(b, NMIX - 1)
                for i in range(1, NCH):
                    if i == NBUF and c is not None:
                        latents_and_bias(c)
                    scan_input(b, i)
                if c is not None:
                    rstd(small_y, "ve3", "rstd3", c)
                rstd(small, "ve2", "rstd2", b)
                rstd(small, "ve1", "rstd1", nxt)

            rstd(small, "ve1", "rstd1", 0)
            turn(0, 1)
            with pool.Fori(1, B) as b:
                turn(b, pool.snap(b + 1), pool.snap(b - 1))
            latents_and_bias(B - 1)
            rstd(small_y, "ve3", "rstd3", B - 1)
            pool.wait_ge(s["w2_loaded"], 32)
            for b in range(B):
                pool.wait_ge(s[f"lat_back{b % BC}"], 16 * (b // BC + 1))
                g.tensor_tensor(lat_all[:, b % BC, :], lat_all[:, b % BC, :], b2_rows[:, :], ALU.add
                                ).then_inc(s["latb2_ready"], 1)

        @block.vector
        def _(dve):
            v = nc.vector
            v.memset(bank[2][:, :], 0.0).then_inc(s["init_dve"], 1)
            v.memset(bank[3][:, :], 0.0).then_inc(s["init_dve"], 1)
            v.memset(dt65[DD:DD + 1, :], 1.0).then_inc(s["init_dve"], 1)
            v.memset(mask_b[:, NCTX:NKEY], 0.0).then_inc(s["init_dve"], 1)
            dve.wait_ge(s["init_dve"], 4)

            def layer_norm(src, n, w, done, b):
                v.bn_stats(stats[:, :], src[:, :]).then_inc(s[f"st{n}"], 1)
                dve.wait_ge(s[f"st{n}"], b + 1)
                v.memset(waiter[:, w:w + 1], 0.0)
                v.bn_aggr(mv[:, :], stats[:, :]).then_inc(s[f"mv{n}"], 1)
                dve.wait_ge(s[f"mv{n}"], b + 1)
                v.tensor_scalar(small[:, 0:1], mv[:, 1:2], EPS_LN, None, ALU.add).then_inc(s[f"ve{n}"], 1)
                dve.wait_ge(s[f"rstd{n}"], b + 1)
                v.tensor_scalar(rows[:, :], src[:, :], mv[:, 0:1], small[:, 1:2], ALU.subtract, ALU.mult
                                ).then_inc(s[done], 1)

            def norm_input(b):
                dve.wait_ge(s["xin_loaded"], 16 * b + 16)
                layer_norm(x_in, 1, 0, "xn_ready", b)

            def shift(b):
                dve.wait_ge(s["xa_ready"], b + 1)
                v.tensor_tensor(sx[:, :, :], xa[:, :, 0:T], xa[:, :, 1:T + 1], ALU.subtract).then_inc(s["sx_ready"], 1)
                dve.wait_ge(s["sx_ready"], b + 1)
                for k in range(NT):
                    i = v.scalar_tensor_tensor(out=xxx[:, k, :], in0=sx[:, k, :], scalar=V["maa_x"][:, k:k + 1],
                                               in1=xa[:, k, 1:T + 1], op0=ALU.mult, op1=ALU.add)
                i.then_inc(s["xxx_ready"], 1)

            def mix(b, j):
                dve.wait_ge(s["m_ready"], b * NMIX + j + 1)
                if j >= 2:
                    dve.wait_ge(s["xj_ready"], b * NMIX + j - 1)
                for k in range(NT):
                    i = v.scalar_tensor_tensor(out=tmp[:, j % 2, k, :], in0=tiles(MIX_BANK[j])[:, k, :],
                                               scalar=V["maa_" + "vkwrg"[j]][:, k:k + 1], in1=sx[:, k, :],
                                               op0=ALU.add, op1=ALU.mult)
                i.then_inc(s["mix_ready"], 1)

            def own_token(b):
                dve.wait_ge(s["rt_ready"], b + 1)
                dve.wait_ge(s["ks_ready"], b + 1)
                for k in range(NT):
                    i = v.scalar_tensor_tensor(out=ruk[:, k, :], in0=ks[:, k, 1:T + 1],
                                               scalar=V["faaaa"][:, k:k + 1], in1=rt[:, k, :],
                                               op0=ALU.mult, op1=ALU.mult)
                i.then_inc(s["ruk_ready"], 1)

            def gating(b):
                dve.wait_ge(s["th_ready"], b + 1)
                v.scalar_tensor_tensor(out=gate[:, :, :], in0=gate[:, :, :], scalar=1.0, in1=tiles(6),
                                       op0=ALU.add, op1=ALU.mult).then_inc(s["gate_ready"], 1)

            def own_values(b):
                dve.wait_ge(s["rkp_ready"], b + 1)
                v.tensor_tensor(ruk[:, :, :], tiles(5), vt[:, :, 1:T + 1], ALU.mult).then_inc(s["y1_ready"], 1)

            def scan_chunk(b, i):
                c, buf = i // 2, scan[i % NBUF]
                dve.wait_ge(s["s0_put"], b * NCH + i + 1)
                dve.wait_ge(s["ws_ready"], b + 1)
                for q in range(VS):
                    n = v.tensor_tensor_scan(buf[:, q, :], ws[:, c, :], buf[:, q, :], 0.0, ALU.mult, ALU.add)
                n.then_inc(s["s_ready"], 1)

            def times_r(b, i):
                c, buf = i // 2, scan[i % NBUF]
                dve.wait_ge(s["rt_ready"], b + 1)
                dve.wait_ge(s["s_ready"], b * NCH + i + 1)
                v.tensor_tensor(buf, buf, rt[:, c:c + 1, :].broadcast_to([P, VS, T]), ALU.mult
                                ).then_inc(s["prod_ready"], 1)

            def group_norm(b):
                yh = y[:, :].rearrange("p (h a) -> p h a", a=S)
                sqh = ysq[:, :].rearrange("p (h a) -> p h a", a=S)

                def per_head(ap):
                    return ap.unsqueeze(2).broadcast_to([T, H, S])
                dve.wait_ge(s["y_ready"], b + 1)
                y_rows = bank[7][0:T, :].rearrange("p (h a) -> p h a", a=S)
                v.tensor_reduce(hs[:, 0, :], y_rows, AX.X, ALU.add).then_inc(s["gsum"], 1)
                dve.wait_ge(s["gsum"], b + 1)
                v.tensor_scalar(hs[:, 1, :], hs[:, 0, :], 1.0 / S, None, ALU.mult).then_inc(s["gmean"], 1)
                dve.wait_ge(s["gmean"], b + 1)
                v.tensor_tensor(yh, y_rows, per_head(hs[:, 1, :]), ALU.subtract).then_inc(s["gcen"], 1)
                dve.wait_ge(s["gcen"], b + 1)
                v.tensor_tensor(sqh, yh, yh, ALU.mult).then_inc(s["gsq"], 1)
                dve.wait_ge(s["gsq"], b + 1)
                v.tensor_reduce(hs[:, 2, :], sqh, AX.X, ALU.add).then_inc(s["gvar"], 1)
                dve.wait_ge(s["gsd"], b + 1)
                v.reciprocal(hs[:, 3, :], hs[:, 0, :]).then_inc(s["grstd"], 1)
                dve.wait_ge(s["grstd"], b + 1)
                v.tensor_tensor(rows[:, :].rearrange("p (h a) -> p h a", a=S), yh, per_head(hs[:, 3, :]), ALU.mult
                                ).then_inc(s["yn_ready"], 1)

            def gated(b):
                dve.wait_ge(s["ya_ready"], b + 1)
                v.scalar_tensor_tensor(out=ruk[:, :, :], in0=ruk[:, :, :], scalar=0.5, in1=gate[:, :, :],
                                       op0=ALU.mult, op1=ALU.mult).then_inc(s["yg_ready"], 1)

            def channel_mix(b):
                dve.wait_ge(s["wo_ready"], b + 1)
                v.tensor_tensor(x2[:, :], x_in[:, :], bank[5][0:T, :], ALU.add).then_inc(s["x2_ready"], 1)
                dve.wait_ge(s["x2_ready"], b + 1)
                layer_norm(x2, 2, 1, "x2n_ready", b)
                dve.wait_ge(s["xc_ready"], b + 1)
                v.tensor_tensor(sx[:, :, :], xa[:, :, 0:T], xa[:, :, 1:T + 1], ALU.subtract
                                ).then_inc(s["sxc_ready"], 1)
                dve.wait_ge(s["sxc_ready"], b + 1)
                for m, w in enumerate(("fmaa_k", "fmaa_r")):
                    for k in range(NT):
                        i = v.scalar_tensor_tensor(out=xj[:, m, k, :], in0=sx[:, k, :], scalar=V[w][:, k:k + 1],
                                                   in1=xa[:, k, 1:T + 1], op0=ALU.mult, op1=ALU.add)
                    i.then_inc(s["xk_ready"], 1)

            def latents(b, nxt, first=False):
                dve.wait_ge(s["kk_relu"], b + 1)
                v.tensor_tensor(tmp[:, 1], tmp[:, 0], tmp[:, 0], ALU.mult).then_inc(s["kk_ready"], 1)
                norm_input(nxt)
                dve.wait_ge(s["rrt_ready"], b + 1)
                dve.wait_ge(s["ffn_ready"], b + 1)
                v.scalar_tensor_tensor(out=ysq[:, :], in0=ysq[:, :], scalar=1.0, in1=bank[6][0:T, :], op0=ALU.add,
                                       op1=ALU.mult).then_inc(s["ffg"], 1)
                dve.wait_ge(s["ffg"], b + 1)
                if not first:
                    dve.wait_ge(s["lat_stored"], b * 16)
                    dve.wait_ge(s["latob_ready"], b)
                v.scalar_tensor_tensor(out=lat[:, :], in0=ysq[:, :], scalar=0.5, in1=x2[:, :], op0=ALU.mult,
                                       op1=ALU.add).then_inc(s["lat_ready"], 1)
                shift(nxt)

            def mask(c):
                dve.wait_ge(s["mask_loaded"], 16 * c + 16)
                v.tensor_scalar(mask_b[:, 0:NCTX], mask_i[:, :], 0.0, MASKED, ALU.is_equal, ALU.mult
                                ).then_inc(s["mask_eq"], 1)

            def head(c, h):
                if h == 0:
                    dve.wait_ge(s["mask_eq"], c + 1)
                if h < NH:
                    dve.wait_ge(s["s_done"], c * NH + h + 1)
                    if h >= 3:
                        dve.wait_ge(s["pt_ready"], c * NH + h - 2)
                    v.memset(waiter[:, h + 2:h + 3], 0.0)
                    v.tensor_tensor_reduce(sm[h % 3], bank[h % 2][0:T, 0:NKEY], mask_b[:, :],
                                           -1.0 / DH, 3e38, ALU.add, ALU.min, nmax[:, h:h + 1]
                                           ).then_inc(s["masked"], 1)
                if h >= 1:
                    g = h - 1
                    dve.wait_ge(s["probs"], c * NH + g + 1)
                    v.reciprocal(rsum[:, 1, g:g + 1], rsum[:, 0, g:g + 1]).then_inc(s["rinv"], 1)
                    dve.wait_ge(s["rinv"], c * NH + g + 1)
                    v.tensor_scalar(sm[g % 3], sm[g % 3], rsum[:, 1, g:g + 1], None, ALU.mult
                                    ).then_inc(s["normed"], 1)

            def rms_norm(c):
                dve.wait_ge(s["op_ready"], c + 1)
                dve.wait_ge(s["latob_ready"], c + 1)
                v.tensor_tensor(x1[:, :], bank[1][0:T, :], lat_ob[:, :], ALU.add).then_inc(s["x1_ready"], 1)
                dve.wait_ge(s["x1_ready"], c + 1)
                v.tensor_tensor_reduce(rows_y[:, :], x1[:, :], x1[:, :], 1.0 / C, EPS_RMS, ALU.mult, ALU.add,
                                       small_y[:, 0:1]).then_inc(s["ve3"], 1)
                dve.wait_ge(s["rstd3"], c + 1)
                v.tensor_scalar(rows_y[:, :], x1[:, :], small_y[:, 1:2], None, ALU.mult).then_inc(s["x1n_ready"], 1)

            def turn(b, nxt, c=None):
                def y_head(*hs_):
                    if c is not None:
                        for h in hs_:
                            head(c, h)
                if c is not None:
                    mask(c)
                mix(b, MIX_V)
                mix(b, MIX_K)
                y_head(0)
                mix(b, MIX_W)
                y_head(1)
                mix(b, MIX_R)
                y_head(2)
                y_head(3)
                mix(b, MIX_G)
                y_head(4)
                scan_chunk(b, 0)
                y_head(5)
                times_r(b, 0)
                own_token(b)
                scan_chunk(b, 1)
                y_head(6)
                times_r(b, 1)
                gating(b)
                y_head(7)
                scan_chunk(b, 2)
                y_head(8)
                times_r(b, 2)
                own_values(b)
                for i in range(3, NCH - 1):
                    y_head(2 * i + 3)
                    scan_chunk(b, i)
                    y_head(2 * i + 4)
                    times_r(b, i)
                scan_chunk(b, NCH - 1)
                times_r(b, NCH - 1)
                group_norm(b)
                if c is not None:
                    rms_norm(c)
                gated(b)
                channel_mix(b)
                latents(b, nxt, first=c is None)

            norm_input(0)
            dve.wait_ge(s["vec_loaded"], 32)
            dve.wait_ge(s["init_pool"], 12)
            shift(0)
            turn(0, 1)
            with dve.Fori(1, B) as b:
                turn(b, dve.snap(b + 1), dve.snap(b - 1))
            mask(B - 1)
            def h1_low(n, first, last):
                dve.wait_ge(s["h1_hi_ready"], n)
                v.tensor_tensor(h1_lo[:, first:last], h1[:, first:last],
                                h1_hi[:, first:last].bitcast(F32), ALU.subtract).then_inc(s["h1_lo_ready"], 1)

            def w1_low(g, p, f):
                dve.wait_ge(s["w1_hi_ready"], g + 1)
                v.tensor_tensor(w1_lo[p][:, :, :], w1[:, bass.ds(f, 1)].rearrange("p f k n -> p (f k) n"),
                                w1_hi[p][:, :, :].bitcast(F32), ALU.subtract).then_inc(s["w1_ready"], 1)

            def w2_low(g, p, f):
                dve.wait_ge(s["w2_hi_ready"], g + 1)
                v.tensor_tensor(w2_lo[p][:, :], w2[:, bass.ds(f, 1)].rearrange("p f n -> p (f n)"),
                                w2_hi[p][:, :].bitcast(F32), ALU.subtract).then_inc(s["w2_ready"], 1)

            def split_hidden(g, p):
                dve.wait_ge(s["hid_ready"], g + 1)
                v.tensor_copy(hid_hi[p][:, :], hid[p]).then_inc(s["hid_hi_ready"], 1)
                dve.wait_ge(s["hid_hi_ready"], g + 1)
                v.tensor_tensor(hid_lo[p][:, :], hid[p], hid_hi[p][:, :].bitcast(F32), ALU.subtract
                                ).then_inc(s["hid_split"], 1)

            for h in range(NH + 1):
                head(B - 1, h)
                if h in (7, 8, 11, 12):
                    n = (7, 8, 11, 12).index(h)
                    h1_low(n + 1, 2 * n, min(2 * n + 2, B - 1))
                if h in (9, 10):
                    w1_low(h - 9, h - 9, h - 9)

            def output_rows(n):
                for b in range(n * BC, (n + 1) * BC):
                    if b % BC < BC - 1:
                        dve.wait_ge(s["mo_ready"], n * (BC - 1) + b % BC + 1)
                    else:
                        dve.wait_ge(s["step_done"], (n + 1) * NF)
                    dve.wait_ge(s["latb2_ready"], b + 1)
                    buf = lat_all[:, b % BC, :]
                    v.tensor_tensor(buf, bank[OUT_BANK[b % BC]][0:T, :], buf, ALU.add).then_inc(s["y2_ready"], 1)

            def step(g, p, last=False):
                split_hidden(g, p)
                if not last:
                    w1_low(g + 2, p, (g + 2) % NF)
                if not last or p == 0:
                    w2_low(g + 1, 1 - p, (g + 1) % NF)

            w2_low(0, 0, 0)
            step(0, 0)
            rms_norm(B - 1)
            step(1, 1)
            h1_low(5, B - 1, B)
            with dve.Fori(1, NF // 2) as i:
                step(dve.snap(2 * i), 0)
                step(dve.snap(2 * i + 1), 1)
            split_hidden(NF, 0)
            output_rows(0)
            w1_low(NF + 2, 0, 2)
            w2_low(NF + 1, 1, 1)
            step(NF + 1, 1)
            with dve.Fori(NF // 2 + 1, NF - 1) as i:
                step(dve.snap(2 * i), 0)
                step(dve.snap(2 * i + 1), 1)
            step(2 * NF - 2, 0, last=True)
            step(2 * NF - 1, 1, last=True)
            output_rows(1)

        @block.scalar
        def _(act):
            c_ = nc.scalar
            act.wait_ge(s["vec_loaded"], 32)
            act.wait_ge(s["init_pool"], 12)
            act.wait_ge(s["queries_zeroed"], 1)

            def columns(dst, src, scale, bias, done):
                for k in range(NT):
                    kw = {"bias": V[bias][:, k:k + 1]}
                    if scale is not None:
                        kw["scale"] = V[scale][:, k:k + 1]
                    i = c_.activation(dst[:, k, :], src[:, k, :], ACT.Identity, **kw)
                i.then_inc(s[done], 1)

            def head(c, i):
                if i < NH:
                    act.wait_ge(s["masked"], c * NH + i + 1)
                    c_.activation(sm[i % 3], sm[i % 3], ACT.Exp, bias=nmax[:, i:i + 1], scale=-1.0,
                                  accum_out=rsum[:, 0, i:i + 1]).then_inc(s["probs"], 1)
                if i >= 2:
                    g = i - 2
                    act.wait_ge(s["pt_ready"], c * NH + g + 1)
                    if g >= 2:
                        act.wait_ge(s["pvh"], c * NH + g - 1)
                    c_.copy(pts[0:KT_ROWS, g % 2], tiles(2 + g % 2)[0:KT_ROWS]).then_inc(s["pt_kept"], 1)

            def query(c):
                act.wait_ge(s["qp_ready"], c + 1)
                for h in range(NH):
                    k, r = h // HG, h % HG * DH
                    i = c_.activation(queries[r:r + DH, h, :], tiles(0)[r:r + DH, k, :], ACT.Identity,
                                      bias=V["q_b"][r:r + DH, k:k + 1])
                i.then_inc(s["qt_ready"], 1)

            def latent_keys(c):
                act.wait_ge(s["kl_ready"], c + 1)
                columns(kt[:, :, NCTX:NKEY], tiles(1), None, "k_b", "ktl_ready")

            def latent_values(c):
                act.wait_ge(s["vl_ready"], c + 1)
                c_.copy(vv[0:T, 3, :], bank[2][0:T, :]).then_inc(s["vvl_ready"], 1)

            def context(b, n):
                act.wait_ge(s["ctx_ready"], b * 7 + n + 1)
                src = bank[CTX_BANK[n]]
                if n < NT:
                    c_.activation(kt[:, n, 0:NCTX], src[:, 0:NCTX], ACT.Identity,
                                  bias=V["k_b"][:, n:n + 1]).then_inc(s["ctx_kept"], 1)
                else:
                    c_.copy(vv[0:KT_ROWS, n - NT, :], src[0:KT_ROWS, :]).then_inc(s["ctx_kept"], 1)

            def attention_output(c):
                act.wait_ge(s["pvh"], c * NH + NH)
                columns(lt, tiles(4), None, "v_b", "ao_ready")

            def mlp_input(c, dst):
                act.wait_ge(s["h1T_ready"], c + 1)
                for k in range(NT):
                    i = c_.activation(dst[:, k, :], tiles(0)[:, k, :], ACT.Copy, scale=V["post_w"][:, k:k + 1])
                i.then_inc(s["h1_ready"], 1)

            def input_columns(b, row):
                c_.copy(xa[:, :, 0:1], shifts[:, bass.ds(row, 1), 1, :].rearrange("p b k -> p k b"))
                act.wait_ge(s["xnT_ready"], b + 1)
                columns(xa[:, :, 1:T + 1], tiles(5), "ln1_w", "ln1_b", "xa_ready")

            def adapter_tanh(b):
                act.wait_ge(s["tp_ready"], b + 1)
                c_.activation(t4[:, 0, :], bank[6][:, 0:T], ACT.Tanh)
                c_.activation(t4[0:DM, 1, :], bank[6][0:DM, T:2 * T], ACT.Tanh).then_inc(s["t_ready"], 1)

            def turn(b, nxt, nxt_row, c=None):
                def y_head(*hs_):
                    if c is not None:
                        for h in hs_:
                            head(c, h)
                if c is not None:
                    query(c)
                if c is not None:
                    latent_keys(c)
                if c is not None:
                    latent_values(c)
                y_head(0)
                act.wait_ge(s["pv_ready"], b + 1)
                c_.copy(vt[:, :, 1:T + 1], tiles(7)).then_inc(s["vt_ready"], 1)
                y_head(1)
                act.wait_ge(s["d1_ready"], b + 1)
                c_.activation(dt65[0:DD, :], bank[6][0:DD, 0:T], ACT.Tanh).then_inc(s["dt_ready"], 1)
                y_head(2)
                act.wait_ge(s["pk_ready"], b + 1)
                c_.copy(ks[:, :, 1:T + 1], tiles(6)).then_inc(s["ks_ready"], 1)
                y_head(3)
                act.wait_ge(s["d2_ready"], b + 1)
                c_.activation(gate[:, :, :], tiles(5), ACT.Exp).then_inc(s["w_exp"], 1)
                act.wait_ge(s["w_exp"], b + 1)
                c_.activation(ws[:, :, 1:T], gate[:, :, 0:T - 1], ACT.Exp, scale=-1.0).then_inc(s["ws_ready"], 1)
                y_head(4)
                act.wait_ge(s["pr_ready"], b + 1)
                c_.copy(rt[:, :, :], tiles(7)).then_inc(s["rt_ready"], 1)
                y_head(5)
                act.wait_ge(s["pg_ready"], b + 1)
                act.wait_ge(s["ws_ready"], b + 1)
                c_.activation(gate[:, :, :], tiles(6), ACT.Tanh, scale=0.5).then_inc(s["th_ready"], 1)
                y_head(*range(6, NH + 2))
                if c is not None:
                    attention_output(c)
                c_.activation(table[:, :], eps[0:1, :], ACT.Sqrt)
                context(b, 0)
                act.wait_ge(s["gvar"], b + 1)
                c_.activation(hs[:, 0, :], hs[:, 2, :], ACT.Sqrt, bias=eps[0:T, :], scale=1.0 / S
                              ).then_inc(s["gsd"], 1)
                context(b, 1)
                context(b, 2)
                act.wait_ge(s["ynT_ready"], b + 1)
                columns(ruk, tiles(6), "gn_w", "gn_b", "ya_ready")
                context(b, 3)
                context(b, 4)
                c_.copy(xa[:, :, 0:1], shifts[:, bass.ds(b, 1), 0, :].rearrange("p b k -> p k b"))
                act.wait_ge(s["xcT_ready"], b + 1)
                columns(xa[:, :, 1:T + 1], tiles(6), "ln2_w", "ln2_b", "xc_ready")
                context(b, 5)
                if c is not None:
                    act.wait_ge(s["h1_stored"], c * 16 + 16)
                    mlp_input(c, h1_out)
                act.wait_ge(s["kkp_ready"], b + 1)
                c_.activation(tmp[:, 0], tiles(7), ACT.Relu).then_inc(s["kk_relu"], 1)
                act.wait_ge(s["rrp_ready"], b + 1)
                c_.activation(ysq[:, :], bank[5][0:T, :], ACT.Tanh, scale=0.5).then_inc(s["rrt_ready"], 1)
                input_columns(nxt, nxt_row)
                context(b, 6)
                act.wait_ge(s["latT_ready"], b + 1)
                c_.copy(lt[:, :, :], tiles(4)).then_inc(s["lt_ready"], 1)
                adapter_tanh(nxt)

            input_columns(0, 0)
            adapter_tanh(0)
            turn(0, 1, 1)
            with act.Fori(1, B) as b:
                turn(b, act.snap(b + 1), act.snap((b + 1) % B), act.snap(b - 1))
            query(B - 1)
            latent_keys(B - 1)
            latent_values(B - 1)
            def h1_high(first, last):
                c_.copy(h1_hi[:, first:last], h1[:, first:last]).then_inc(s["h1_hi_ready"], 1)

            def w1_high(p, f):
                c_.copy(w1_hi[p][:, :, :], w1[:, bass.ds(f, 1)].rearrange("p f k n -> p (f k) n")
                        ).then_inc(s["w1_hi_ready"], 1)

            def w2_high(p, f):
                c_.copy(w2_hi[p][:, :], w2[:, bass.ds(f, 1)].rearrange("p f n -> p (f n)")
                        ).then_inc(s["w2_hi_ready"], 1)

            for i in range(NH + 2):
                head(B - 1, i)
                if i == 6:
                    act.wait_ge(s["mlp_loaded"], 48)
                if i in (6, 7, 10, 11):
                    n = (6, 7, 10, 11).index(i)
                    h1_high(2 * n, min(2 * n + 2, B - 1))
                if i in (8, 9):
                    if i == 8:
                        act.wait_ge(s["xnT_ready"], B + 1)
                        act.wait_ge(s["lat_ready"], B)
                    w1_high(i - 8, i - 8)
            attention_output(B - 1)
            act.wait_ge(s["w2_loaded"], 32)
            act.wait_ge(s["ctx_loaded"], 16 * (B + 1))
            w2_high(0, 0)

            def step(g, p, first=False, last=False):
                act.wait_ge(s["hp_ready"], g + 1)
                if not first:
                    act.wait_ge(s["step_done"], g - 1)
                c_.activation(hid[p], bank[HID_BANK[p]][:, 0:BC * T], ACT.Gelu_apprx_tanh,
                              bias=b1v[:, bass.ds(g % NF, 1)]).then_inc(s["hid_ready"], 1)
                if not last:
                    w1_high(p, (g + 2) % NF)
                if not last or p == 0:
                    if not first or p == 1:
                        act.wait_ge(s["step_done"], g)
                    w2_high(1 - p, (g + 1) % NF)

            step(0, 0, first=True)
            step(1, 1, first=True)
            mlp_input(B - 1, h1[:, B - 1])
            act.wait_ge(s["h1_ready"], B)
            h1_high(B - 1, B)
            with act.Fori(1, NF - 1) as i:
                step(act.snap(2 * i), 0)
                step(act.snap(2 * i + 1), 1)
            step(2 * NF - 2, 0, last=True)
            step(2 * NF - 1, 1, last=True)

        @block.tensor
        def _(pe):
            t_ = nc.tensor

            def turned(dst, src, done):
                for k in range(NT):
                    i = t_.transpose(tiles(dst)[:, k, :], src[:, k * P:(k + 1) * P], ident[0:T, 0:T])
                i.then_inc(s[done], 1)

            def to_columns(dst, w, x, done):
                for m in range(NT):
                    for k in range(NT):
                        i = t_.matmul(tiles(dst)[:, m, :], w[:, k, m * P:(m + 1) * P], x[:, k, :],
                                      start=k == 0, stop=k == NT - 1)
                i.then_inc(s[done], 1)

            def to_rows(dst, w, x, done, m=T):
                for k in range(NT):
                    i = t_.matmul(bank[dst][0:m, :], x[:, k, :], w[:, k, :], start=k == 0, stop=k == NT - 1)
                i.then_inc(s[done], 1)

            def adapter_inputs(b):
                pe.wait_ge(s["xxx_ready"], b + 1)
                for k in range(NT):
                    t_.matmul(bank[6][:, 0:T], maa1[:, k, 0:P], xxx[:, k, :], start=k == 0, stop=k == NT - 1)
                for k in range(NT):
                    i = t_.matmul(bank[6][0:DM, T:2 * T], maa1[:, k, P:P + DM], xxx[:, k, :],
                                  start=k == 0, stop=k == NT - 1)
                i.then_inc(s["tp_ready"], 1)

            def adapter(j):
                r = j % 4 * DM
                for m in range(NT):
                    i = t_.matmul(tiles(MIX_BANK[j])[:, m, :], maa2[r:r + DM, j // 4, m * P:(m + 1) * P],
                                  t4[r:r + DM, j // 4, :], start=True, stop=True)
                i.then_inc(s["m_ready"], 1)

            def context(b, n):
                if n == 0:
                    pe.wait_ge(s["ctx_loaded"], 16 * b + 16)
                if n >= 2:
                    pe.wait_ge(s["ctx_kept"], b * 7 + n - 1)
                dst = bank[CTX_BANK[n]]
                for k in range(NT):
                    if n < NT:
                        i = t_.matmul(dst[:, 0:NCTX], W["kw"][:, k, n * P:(n + 1) * P], ctxt[:, k, :],
                                      start=k == 0, stop=k == NT - 1)
                    else:
                        r = (n - NT) * KT_ROWS
                        i = t_.matmul(dst[0:KT_ROWS, :], ctxt[:, k, r:r + KT_ROWS], W["vw"][:, k, :],
                                      start=k == 0, stop=k == NT - 1)
                i.then_inc(s["ctx_ready"], 1)

            def sum_chunk(b, i):
                pe.wait_ge(s["prod_ready"], b * NCH + i + 1)
                y_chunk = bank[7][0:T, i // 2 * P:(i // 2 + 1) * P].rearrange("p (h a) -> p h a", a=S)
                for q in range(VS):
                    n = t_.matmul(y_chunk[:, :, i % 2 * VS:(i % 2 + 1) * VS], scan[i % NBUF][:, q, :],
                                  place[:, VS - 1 - q:VS - 1 - q + HT * VS], start=i == 0 and q == 0, stop=False)
                n.then_inc(s["yacc_ready"], 1)

            def head(c, i):
                if i < NH:
                    if i >= 2:
                        pe.wait_ge(s["masked"], c * NH + i - 1)
                    t_.matmul(bank[i % 2][0:T, 0:NKEY], queries[:, i, :], kt[:, i // HG, :],
                              start=True, stop=True).then_inc(s["s_done"], 1)
                if 2 <= i < NH + 2:
                    g = i - 2
                    pe.wait_ge(s["normed"], c * NH + g + 1)
                    if g >= 2:
                        pe.wait_ge(s["pt_kept"], c * NH + g - 1)
                    for j in range(NKT):
                        n = KT_ROWS if j < 3 else T
                        m = t_.transpose(tiles(2 + g % 2)[0:n, j, :], sm[g % 3][:, j * KT_ROWS:j * KT_ROWS + n],
                                         ident[0:T, 0:T])
                    m.then_inc(s["pt_ready"], 1)
                if i >= 3:
                    g = i - 3
                    pe.wait_ge(s["pt_kept"], c * NH + g + 1)
                    for j in range(NKT):
                        n = KT_ROWS if j < 3 else T
                        r = g % HG * DH
                        m = t_.matmul(tiles(4)[r:r + DH, g // HG, :], vv[0:n, j, g * DH:(g + 1) * DH],
                                      pts[0:n, g % 2, j, :], start=j == 0, stop=j == NKT - 1)
                    m.then_inc(s["pvh"], 1)

            def query(c):
                pe.wait_ge(s["lt_ready"], c + 1)
                to_columns(0, W["qw"], lt, "qp_ready")

            def before_heads(c):
                pe.wait_ge(s["qt_ready"], c + 1)
                pe.wait_ge(s["ktl_ready"], c + 1)
                pe.wait_ge(s["vvl_ready"], c + 1)
                pe.wait_ge(s["ctx_kept"], c * 7 + 7)

            def output_projection(c):
                pe.wait_ge(s["ao_ready"], c + 1)
                to_rows(1, W["ow"], lt, "op_ready")

            def mlp_input(c):
                pe.wait_ge(s["x1n_ready"], c + 1)
                turned(0, rows_y, "h1T_ready")

            def input_turned(b):
                pe.wait_ge(s["xn_ready"], b + 1)
                turned(5, rows, "xnT_ready")

            def turn(b, nxt, c=None):
                def y_head(*hs_):
                    if c is not None:
                        for h in hs_:
                            head(c, h)
                if c is not None:
                    query(c)
                if c is not None:
                    to_columns(1, W["kw"], lt, "kl_ready")
                if c is not None:
                    to_rows(2, W["vw"], lt, "vl_ready")
                pe.wait_ge(s["t_ready"], b + 1)
                adapter(MIX_V)
                adapter(MIX_K)
                if c is not None:
                    before_heads(c)
                y_head(0)
                adapter(MIX_W)
                if c is None:
                    pe.wait_ge(s["wv_loaded"], 16)
                pe.wait_ge(s["xj_ready"], b * NMIX + MIX_V + 1)
                to_columns(7, W["Wv"], xj[:, MIX_V % 3], "pv_ready")
                y_head(1)
                pe.wait_ge(s["mix_ready"], b * NMIX + MIX_K + 1)
                adapter(MIX_R)
                pe.wait_ge(s["mix_ready"], b * NMIX + MIX_W + 1)
                pe.wait_ge(s["xj_ready"], b * NMIX + MIX_W + 1)
                for k in range(NT):
                    i = t_.matmul(bank[6][0:DD, 0:T], dec1[:, k, :], xj[:, MIX_W % 3, k, :],
                                  start=k == 0, stop=k == NT - 1)
                i.then_inc(s["d1_ready"], 1)
                y_head(2)
                pe.wait_ge(s["dt_ready"], b + 1)
                if c is None:
                    pe.wait_ge(s["weights_loaded"], 16)
                to_columns(6, W["Wk"], xj[:, MIX_K % 3], "pk_ready")
                y_head(3)
                pe.wait_ge(s["vt_ready"], b + 1)
                adapter(MIX_G)
                pe.wait_ge(s["mix_ready"], b * NMIX + MIX_R + 1)
                for m in range(NT):
                    i = t_.matmul(tiles(5)[:, m, :], dec2[:, m * P:(m + 1) * P], dt65[:, :], start=True, stop=True)
                i.then_inc(s["d2_ready"], 1)
                y_head(4)
                pe.wait_ge(s["mix_ready"], b * NMIX + MIX_G + 1)
                pe.wait_ge(s["xj_ready"], b * NMIX + MIX_R + 1)
                to_columns(7, W["Wr"], xj[:, MIX_R % 3], "pr_ready")
                y_head(5)
                pe.wait_ge(s["ks_ready"], b + 1)
                pe.wait_ge(s["xj_ready"], b * NMIX + MIX_G + 1)
                to_columns(6, W["Wg"], xj[:, MIX_G % 3], "pg_ready")
                y_head(6)
                pe.wait_ge(s["rt_ready"], b + 1)
                sum_chunk(b, 0)
                y_head(7)
                pe.wait_ge(s["ruk_ready"], b + 1)
                pe.wait_ge(s["w_exp"], b + 1)
                for k in range(NT):
                    i = t_.matmul(tiles(5)[:, k, :], same_head[:, :], ruk[:, k, :], start=True, stop=True)
                i.then_inc(s["rkp_ready"], 1)
                y_head(8)
                sum_chunk(b, 1)
                y_head(9, 10)
                sum_chunk(b, 2)
                if c is None:
                    pe.wait_ge(s["kvw_loaded"], 16)
                    context(b, 0)
                y_head(11, 12)
                sum_chunk(b, 3)
                y_head(13, 14)
                sum_chunk(b, 4)
                if c is None:
                    context(b, 1)
                y_head(15, 16)
                sum_chunk(b, 5)
                y_head(17)
                sum_chunk(b, 6)
                if c is not None:
                    context(b, 0)
                y_head(18)
                sum_chunk(b, 7)
                if c is not None:
                    output_projection(c)
                pe.wait_ge(s["y1_ready"], b + 1)
                for k in range(NT):
                    i = t_.matmul(bank[7][0:T, k * P:(k + 1) * P], ruk[:, k, :], ident[:, :],
                                  start=False, stop=k == NT - 1)
                i.then_inc(s["y_ready"], 1)
                if c is not None:
                    context(b, 1)
                context(b, 2)
                pe.wait_ge(s["gate_ready"], b + 1)
                pe.wait_ge(s["yn_ready"], b + 1)
                turned(6, rows, "ynT_ready")
                context(b, 3)
                pe.wait_ge(s["yg_ready"], b + 1)
                if c is None:
                    pe.wait_ge(s["wlate_loaded"], 16 * LATE)
                to_rows(5, W["Wo"], ruk, "wo_ready")
                context(b, 4)
                pe.wait_ge(s["x2n_ready"], b + 1)
                turned(6, rows, "xcT_ready")
                context(b, 5)
                if c is not None:
                    mlp_input(c)
                pe.wait_ge(s["xk_ready"], 2 * b + 1)
                to_columns(7, W["fWk"], xj[:, 0], "kkp_ready")
                pe.wait_ge(s["xk_ready"], 2 * b + 2)
                to_rows(5, W["fWr"], xj[:, 1], "rrp_ready")
                pe.wait_ge(s["kk_ready"], b + 1)
                to_rows(6, W["fWv"], tmp[:, 1], "ffn_ready")
                pe.wait_ge(s["rrt_ready"], b + 1)
                input_turned(nxt)
                context(b, 6)
                pe.wait_ge(s["lat_ready"], b + 1)
                turned(4, lat, "latT_ready")
                adapter_inputs(nxt)

            pe.wait_ge(s["init_pool"], 12)
            pe.wait_ge(s["init_dve"], 4)
            input_turned(0)
            pe.wait_ge(s["const_loaded"], 16 * 6)
            adapter_inputs(0)
            turn(0, 1)
            with pe.Fori(1, B) as b:
                turn(b, pe.snap(b + 1), pe.snap(b - 1))
            query(B - 1)
            to_columns(1, W["kw"], lt, "kl_ready")
            to_rows(2, W["vw"], lt, "vl_ready")
            before_heads(B - 1)
            def hidden_product(n, g, p, first=False):
                pe.wait_ge(s["w1_ready"], g + 1)
                if not first:
                    pe.wait_ge(s["hid_ready"], g - 1)
                wh, wl = w1_hi[p], w1_lo[p]
                for k in range(NT):
                    for w, x in ((wh, h1_hi), (wh, h1_lo), (wl, h1_hi)):
                        i = t_.matmul(bank[HID_BANK[p]][:, 0:BC * T], w[:, k, :], x[:, n * BC:(n + 1) * BC, k, :],
                                      start=k == 0 and w is wh and x is h1_hi, stop=k == NT - 1 and w is wl)
                i.then_inc(s["hp_ready"], 1)

            def output_products(n, g, p, start=False, stop=False):
                pe.wait_ge(s["hid_split"], g + 1)
                pe.wait_ge(s["w2_ready"], g + 1)
                xh, xl, wh, wl = hid_hi[p], hid_lo[p], w2_hi[p], w2_lo[p]
                for b in range(BC):
                    if n and start:
                        pe.wait_ge(s["y2_ready"], b + 1)
                    for x, w in ((xh, wh), (xh, wl), (xl, wh)):
                        i = t_.matmul(bank[OUT_BANK[b]][0:T, :], x[:, b * T:(b + 1) * T], w[:, :],
                                      start=start and x is xh and w is wh, stop=stop and x is xl)
                    if b == BC - 1:
                        i.then_inc(s["step_done"], 1)
                    elif stop:
                        i.then_inc(s["mo_ready"], 1)

            for i in range(NH + 3):
                head(B - 1, i)
                if i == 16:
                    pe.wait_ge(s["h1_lo_ready"], 2)
                    pe.wait_ge(s["xa_ready"], B + 1)
                    pe.wait_ge(s["t_ready"], B + 1)
                    hidden_product(0, 0, 0, first=True)
                if i == 18:
                    hidden_product(0, 1, 1, first=True)
            output_projection(B - 1)
            for n in range(2):
                g = n * NF
                output_products(n, g, 0, start=True)
                if n == 0:
                    mlp_input(B - 1)
                hidden_product(n, g + 2, 0)
                output_products(n, g + 1, 1)
                hidden_product(n, g + 3, 1)
                with pe.Fori(g // 2 + 1, g // 2 + NF // 2 - 1) as i:
                    for p in range(2):
                        output_products(n, pe.snap(2 * i + p), p)
                        hidden_product(n, pe.snap(2 * i + p + 2), p)
                output_products(n, g + NF - 2, 0)
                if n == 0:
                    pe.wait_ge(s["h1_lo_ready"], 5)
                    hidden_product(1, NF, 0)
                output_products(n, g + NF - 1, 1, stop=True)
                if n == 0:
                    hidden_product(1, NF + 1, 1)


def kernel(**inputs):
    import numpy as np
    import concourse.bacc as bacc
    from concourse.bass_utils import run_bass_kernel_spmd as run

    i = {k: np.asarray(v) for k, v in inputs.items()}
    L0 = {k[len("L0_xattn_"):]: v for k, v in i.items() if k.startswith("L0_xattn_")}
    L1 = {k[len("L1_xattn_"):]: v for k, v in i.items() if k.startswith("L1_xattn_")}

    def cols(v):
        return v.reshape(-1, P).T

    def wt(w):
        return w.reshape(-1, P, w.shape[1]).transpose(1, 0, 2)

    kv_w = L1["kv_w"].reshape(C, C, 2)
    kv_b = L1["kv_b"].reshape(C, 2)
    vecs = dict(ln1_w=L0["ln1_w"], ln1_b=L0["ln1_b"], ln2_w=L0["ln2_w"], ln2_b=L0["ln2_b"], maa_x=L0["maa_x"],
                faaaa=L0["faaaa"].reshape(C), gn_w=L0["gn_w"], gn_b=L0["gn_b"], fmaa_k=L0["fmaa_k"],
                fmaa_r=L0["fmaa_r"], q_b=L1["q_b"], k_b=kv_b[:, 0], v_b=kv_b[:, 1], post_w=L1["postnorm_w"],
                **{"maa_" + n: L0["maa_" + n] for n in "vkwrg"})
    big = dict(Wv=L0["Wv"].T, Wk=L0["Wk"].T, Wr=L0["Wr"].T, Wg=L0["Wg"].T, Wo=L0["Wo"].T, fWk=L0["fWk"].T,
               fWr=L0["fWr"].T, fWv=L0["fWv"].T, kw=kv_w[:, :, 0], vw=kv_w[:, :, 1], qw=L1["q_w"], ow=L1["out_w"])
    order = [2, 1, 0, 3, 4]
    maa1 = L0["maa_w1"].reshape(C, NMIX, DM)[:, order].reshape(C, NMIX * DM)
    c = i["ctx_2048"]
    arrays = dict(
        x=i["x"],
        vec=np.stack([cols(vecs[n]) for n in VECS], 1),
        shifts=c[:, 0:2].reshape(B, 2, NT, P).transpose(3, 0, 1, 2),
        s0=c[:, 2:2 + S].reshape(B, NT, P, S).transpose(2, 1, 0, 3),
        ctxt=c.reshape(B, NCTX, NT, P).transpose(0, 3, 2, 1),
        mask=i["mask_BxS2_ik0"],
        maa1=wt(maa1),
        maa2=L0["maa_w2"][order].reshape(NMIX * DM, C),
        dec1=wt(L0["decay_w1"]),
        dec2=np.concatenate([L0["decay_w2"], L0["time_decay"][None]], 0),
        wbig=np.stack([wt(big[n]) for n in BIG], 1),
        w1=wt(L1["mlp_w1"]).reshape(P, NT, NF, P).transpose(0, 2, 1, 3), w2=wt(L1["mlp_w2"]), b1=cols(L1["mlp_b1"]),
        b2=L1["mlp_b2"][None], out_b=L1["out_b"][None],
    )
    nc = bacc.Bacc("TRN2", target_bir_lowering=False, num_devices=1)
    feed, aps = {}, {}
    for n, v in arrays.items():
        feed[f"in_{n}"] = np.ascontiguousarray(v)
        aps[n] = nc.dram_tensor(f"in_{n}", v.shape, mybir.dt.from_np(v.dtype), kind="ExternalInput").ap()
    out = nc.dram_tensor("out_0", (B, T, C), F32, kind="ExternalOutput").ap()
    build(nc, aps, out)
    r = run(nc, [feed], core_ids=[0])
    return r.results[0]["out_0"]
```
